# Optimizing a Trainium2 kernel written in Bass

```python
import numpy as np
import jax
import jax.numpy as jnp

def _softmax(x, axis=-1):
    return jax.nn.softmax(x, axis=axis)

def _gelu(x):
    return jax.nn.gelu(x, approximate=True)

def _silu(x):
    return jax.nn.silu(x)

def _sigmoid(x):
    return jax.nn.sigmoid(x)

def _layernorm(x, axis=-1, eps=1e-05):
    m = jnp.mean(x, axis=axis, keepdims=True)
    v = jnp.var(x, axis=axis, keepdims=True)
    return (x - m) / jnp.sqrt(v + eps)

def _scatter_add(tgt, idx, src, axis=0):
    return tgt.at[idx].add(src)

def _segment_sum(src, seg, n):
    return jax.ops.segment_sum(src, seg, n)
kernel_name = 'mk_recurrent_d1_jaxref_r8_281d79'

def setup_inputs(seed: int=0):
    np.random.seed(seed)
    _w = jnp.asarray

    def _L0_attn_setup():
        import math
        import jax, jax.numpy as jnp
        import numpy as np
        E = 128
        H = 16
        DH = E // H
        R = 8
        ALPHA = 16
        LORA_S = ALPHA / R

        def build_slopes(h):
            start = 2 ** (-2 ** (-(math.log2(h) - 3)))
            return jnp.asarray([start * start ** i for i in range(h)], dtype=jnp.float32)

        def _lora(x, W, A, Bm):
            return x @ W.T + x @ Bm.T @ A.T * LORA_S
        key = jax.random.key(seed)
        ks = jax.random.split(key, 12)
        B, T = (2, 256)
        x = jax.random.normal(ks[0], (B, T, E), dtype=jnp.float32)

        def lin(k):
            return jax.random.normal(k, (E, E), dtype=jnp.float32) / math.sqrt(E)
        inp = {'x': x, 'Wq': lin(ks[1]), 'Aq': jax.random.normal(ks[2], (E, R)) * 0.01, 'Bq': jax.random.normal(ks[3], (R, E)) * 0.01, 'Wk': lin(ks[4]), 'Ak': jax.random.normal(ks[5], (E, R)) * 0.01, 'Bk': jax.random.normal(ks[6], (R, E)) * 0.01, 'Wv': lin(ks[7]), 'Av': jax.random.normal(ks[8], (E, R)) * 0.01, 'Bv': jax.random.normal(ks[9], (R, E)) * 0.01, 'Wp': lin(ks[10])}
        return inp
    _L0_attn_in = _L0_attn_setup()

    def _L0_ffn_setup():
        import jax, jax.numpy as jnp
        import numpy as np
        E, D, H = (8, 128, 512)
        B, S = (4, 512)
        TEMPERATURE = 1.0
        key = jax.random.key(seed)
        ks = jax.random.split(key, 7)
        sc = 0.02
        return {'x': jax.random.normal(ks[0], (B, S, D), dtype=jnp.float32), 'W1': jax.random.normal(ks[1], (E, D, H), dtype=jnp.float32) * sc, 'b1': jax.random.normal(ks[2], (E, H), dtype=jnp.float32) * sc, 'W2': jax.random.normal(ks[3], (E, H, D), dtype=jnp.float32) * sc, 'b2': jax.random.normal(ks[4], (E, D), dtype=jnp.float32) * sc, 'Wr': jax.random.normal(ks[5], (D, E), dtype=jnp.float32) * sc, 'br': jax.random.normal(ks[6], (E,), dtype=jnp.float32) * sc}
    _L0_ffn_in = _L0_ffn_setup()
    _d = {'L0_attn_x': _L0_attn_in['x'], 'L0_attn_Wq': _L0_attn_in['Wq'], 'L0_attn_Aq': _L0_attn_in['Aq'], 'L0_attn_Bq': _L0_attn_in['Bq'], 'L0_attn_Wk': _L0_attn_in['Wk'], 'L0_attn_Ak': _L0_attn_in['Ak'], 'L0_attn_Bk': _L0_attn_in['Bk'], 'L0_attn_Wv': _L0_attn_in['Wv'], 'L0_attn_Av': _L0_attn_in['Av'], 'L0_attn_Bv': _L0_attn_in['Bv'], 'L0_attn_Wp': _L0_attn_in['Wp'], 'L0_ffn_W1': _L0_ffn_in['W1'], 'L0_ffn_b1': _L0_ffn_in['b1'], 'L0_ffn_W2': _L0_ffn_in['W2'], 'L0_ffn_b2': _L0_ffn_in['b2'], 'L0_ffn_Wr': _L0_ffn_in['Wr'], 'L0_ffn_br': _L0_ffn_in['br']}
    _x0 = _d['L0_attn_x']
    _d['L0_attn_x'] = jax.random.normal(jax.random.fold_in(jax.random.key(seed), 1), (16, 256, 128), dtype=_x0.dtype)
    del _x0
    return _d

def reference(L0_attn_x, L0_attn_Wq, L0_attn_Aq, L0_attn_Bq, L0_attn_Wk, L0_attn_Ak, L0_attn_Bk, L0_attn_Wv, L0_attn_Av, L0_attn_Bv, L0_attn_Wp, L0_ffn_W1, L0_ffn_b1, L0_ffn_W2, L0_ffn_b2, L0_ffn_Wr, L0_ffn_br):

    def _L0_attn_ref(x, Wq, Aq, Bq, Wk, Ak, Bk, Wv, Av, Bv, Wp):
        import math
        import jax, jax.numpy as jnp
        import numpy as np
        E = 128
        H = 16
        DH = E // H
        R = 8
        ALPHA = 16
        LORA_S = ALPHA / R

        def build_slopes(h):
            start = 2 ** (-2 ** (-(math.log2(h) - 3)))
            return jnp.asarray([start * start ** i for i in range(h)], dtype=jnp.float32)

        def _lora(x, W, A, Bm):
            return x @ W.T + x @ Bm.T @ A.T * LORA_S
        B, T, _ = x.shape
        slopes = build_slopes(H)
        q = _lora(x, Wq, Aq, Bq).reshape(B, T, H, DH).transpose(0, 2, 1, 3)
        k = _lora(x, Wk, Ak, Bk).reshape(B, T, H, DH).transpose(0, 2, 1, 3)
        v = _lora(x, Wv, Av, Bv).reshape(B, T, H, DH).transpose(0, 2, 1, 3)
        s = jnp.einsum('bhqd,bhkd->bhqk', q, k) / math.sqrt(DH)
        i = jnp.arange(T, dtype=jnp.float32)[:, None]
        j = jnp.arange(T, dtype=jnp.float32)[None, :]
        alibi = slopes[:, None, None] * (i - j)
        mask = jnp.triu(jnp.full((T, T), -jnp.inf, dtype=jnp.float32), 1)
        s = s + alibi[None] + mask
        p = jax.nn.softmax(s, axis=-1)
        o = jnp.einsum('bhqk,bhkd->bhqd', p, v).transpose(0, 2, 1, 3).reshape(B, T, E)
        return o @ Wp.T

    def _L0_ffn_ref(x, W1, b1, W2, b2, Wr, br):
        import jax, jax.numpy as jnp
        import numpy as np
        E, D, H = (8, 128, 512)
        B, S = (4, 512)
        TEMPERATURE = 1.0
        routing_logits = (x @ Wr + br) / TEMPERATURE
        routing_probs = jax.nn.softmax(routing_logits, axis=-1)
        indices = jnp.argmax(routing_probs, axis=-1)
        out = jnp.zeros_like(x)
        num_experts = W1.shape[0]
        for i in range(num_experts):
            mask = (indices == i).astype(x.dtype)[..., None]
            xi = x * mask
            h = jax.nn.relu(xi @ W1[i] + b1[i])
            out = out + (h @ W2[i] + b2[i])
        return out
    x = L0_attn_x
    xn = _layernorm(x, axis=-1)
    s = _L0_attn_ref(xn, L0_attn_Wq, L0_attn_Aq, L0_attn_Bq, L0_attn_Wk, L0_attn_Ak, L0_attn_Bk, L0_attn_Wv, L0_attn_Av, L0_attn_Bv, L0_attn_Wp)
    g = _silu(_L0_ffn_ref(xn, L0_ffn_W1, L0_ffn_b1, L0_ffn_W2, L0_ffn_b2, L0_ffn_Wr, L0_ffn_br))
    x = x + s * g
    return x

_drawn_inputs = setup_inputs


def setup_inputs(seed=0):
    import zlib

    import numpy as np

    out = dict(_drawn_inputs(seed))
    spreads = {}
    factors = {'L0_attn_Wq': 4.934,
     'L0_attn_Aq': 8.0,
     'L0_attn_Bq': 8.0,
     'L0_attn_Wk': 4.923,
     'L0_attn_Ak': 8.0,
     'L0_attn_Bk': 8.0,
     'L0_attn_Wv': 3.215,
     'L0_attn_Av': 8.0,
     'L0_attn_Bv': 8.0,
     'L0_attn_Wp': 3.233,
     'L0_ffn_W1': 5.006,
     'L0_ffn_b1': 8.0,
     'L0_ffn_W2': 4.081,
     'L0_ffn_b2': 5.131,
     'L0_ffn_Wr': 4.564,
     'L0_ffn_br': 8.0}
    for name, (base, spread) in spreads.items():
        noise = np.random.default_rng([zlib.crc32(name.encode()), seed]).standard_normal(out[name].shape)
        drawn = base * np.exp(spread * noise) if base else spread * noise
        out[name] = jnp.asarray(drawn.astype(out[name].dtype))
    for name, factor in factors.items():
        out[name] = (out[name] * factor).astype(out[name].dtype)
    return out
```

```python
from contextlib import ExitStack

import numpy as np
import concourse.bass as bass
import concourse.mybir as mybir

F32 = mybir.dt.float32
BF16 = mybir.dt.bfloat16
I32 = mybir.dt.int32
U32 = mybir.dt.uint32
ALU = mybir.AluOpType
ACT = mybir.ActivationFunctionType
AX = mybir.AxisListType

P = 128
NB, T, D = 16, 256, 128
NT = NB * T // P
H, DH = 16, 8
NP = H // 2
BLK = 64
NBLK = T // BLK
RANK = 8
LORA_SCALE = 16 / RANK
E, HID = 8, 512
NC_H = HID // P
WE = HID + NC_H * D + NC_H
SLOT_TILES = (NB * T + E * (P - 1)) // P
EPS = 1e-5
NEG = -1e30

TERMS_Q = ((0, 3), (1, 2), (2, 1))
TERMS_K = ((0, 1, 2), (0, 1), (0,))
CONST_ROW = 48
MAX_ROW = 54
LOADS = 2 * (6 + 3)

UNITS = ([(3, (p, p + 1)) for p in range(0, NP, 2)] + [(2, (p, p + 1)) for p in range(0, NP, 2)]
         + [(1, tuple(range(p, p + 4))) for p in (0, 4)] + [(0, tuple(range(NP)))])
NU = len(UNITS)
PV_AFTER = {1: (0, 1), 3: (2, 3), 5: (4, 5), 7: (6, 7), 8: (8,), 9: (9,), 10: (10,)}
NPV = len(PV_AFTER)


def program(nc, x, wq_t, wk_t, wv_t, aq_t, ak_t, av_t, bq, bk, bv, wp_t, wr, br,
            w_experts, b2, const_f32, const_bf16, q_const_rows, k_const_rows, out):
    x_tiles = x.rearrange("b (k j i) d -> b j i k d", k=NBLK, j=2)
    out_tiles = out.rearrange("b (k j i) d -> b j i k d", k=NBLK, j=2)
    qk_dram = nc.dram_tensor("qk_parts", [NB, 3, 2, P, T], BF16).ap()
    xs_dram = nc.dram_tensor("sorted_rows", [SLOT_TILES * P, D], F32).ap()
    y_dram = nc.dram_tensor("expert_rows", [SLOT_TILES * P, D], F32).ap()

    const_bf16, q_const_rows, k_const_rows = (a.bitcast(BF16) for a in (const_bf16, q_const_rows, k_const_rows))

    ctx = ExitStack()
    with ctx:
        def sb(name, shape, dt=F32):
            return ctx.enter_context(nc.sbuf_tensor(name, shape, dt))

        def sem(name):
            return ctx.enter_context(nc.semaphore(name))

        bank = [ctx.enter_context(nc.psum_tensor(f"bank{i}", [P, 512], F32)) for i in range(8)]

        cf = sb("cf", [P, 2 * P + 64])
        ident_f = cf[:, 0:P]
        ones_f = cf[:, P:2 * P]
        iota8 = cf[:, 2 * P:2 * P + 8]
        iota_tile = cf[0:1, 2 * P + 8:2 * P + 8 + SLOT_TILES]
        of_half = cf[:, 2 * P + 50:2 * P + 52]
        cb = sb("cb", [P, 2 * BLK + 3 * P], BF16)
        mask_qk = cb[:, 0:BLK]
        mask_kq = cb[:, BLK:2 * BLK]
        ident_b = cb[:, 2 * BLK:2 * BLK + P]
        before_b = cb[:, 2 * BLK + P:2 * BLK + 2 * P]
        ones_b = cb[:, 2 * BLK + 2 * P:2 * BLK + 3 * P]
        w_raw = sb("w_raw", [P, 3, P])
        w_eff = sb("w_eff", [P, 3, P])
        lora_a = sb("lora_a", [RANK, 3, P])
        lora_b = sb("lora_b", [RANK, 3, P])
        wp_sb = sb("wp_sb", [P, D])
        wr_sb = sb("wr_sb", [P, E])
        br_sb = sb("br_sb", [P, E])
        b2_sb = sb("b2_sb", [E, D])

        x_all = sb("x_all", [P, NT, D])
        xn_all = sb("xn_all", [P, NT, D])
        v_all = sb("v_all", [P, NB, NBLK, NP, DH])
        s_all = sb("s_all", [P, NT, D])
        stats = sb("stats", [P, NT, 6])
        ln = sb("ln", [P, 8, NT])
        rstd, nmr = sb("rstd", [P, NT]), sb("nmr", [P, NT])
        xn_slot = sb("xn_slot", [P, 2, 2, D])
        xnT_slot = sb("xnT_slot", [P, 2, T])
        parts = sb("parts", [P, 2, 3, 2, T], BF16)
        rem = sb("rem", [P, 2, 2 * T])

        logits = sb("logits", [P, NT, E])
        onehot_b = sb("onehot_b", [P, NT, E], BF16)
        r32 = sb("r32", [P, 4, NT])
        r8 = sb("r8", [P, 8, E])
        r8i = sb("r8i", [P, 2, E], I32)
        slot_of = sb("slot_of", [P, NT], U32)
        te_cmp = sb("te_cmp", [1, SLOT_TILES, E])
        te_f = sb("te_f", [1, 2, SLOT_TILES])
        tile_expert = sb("tile_expert", [1, SLOT_TILES], I32)

        q_plain = [sb(f"q_plain{r}", [P, NP, T], BF16) for r in range(2)]
        k_plain = [sb(f"k_plain{r}", [P, NP, T], BF16) for r in range(2)]
        q_diag = [sb(f"q_diag{r}", [P, NP, 2, T], BF16) for r in range(2)]
        k_diag = [sb(f"k_diag{r}", [P, NP, 2, T], BF16) for r in range(2)]
        v_diag = [sb(f"v_diag{r}", [P, NBLK, NP, 32]) for r in range(2)]
        v_halves = [v[:, :, :, :].rearrange("p n h (c d) -> p (n h) c d", c=2) for v in v_diag]
        probs = sb("probs", [P, NU, 512])
        row_max = [sb(f"row_max{r}", [P, NBLK, NP]) for r in range(2)]
        nmax = [sb(f"nmax{r}", [P, NBLK, 3, NP], BF16) for r in range(2)]
        nmax_rem = sb("nmax_rem", [P, NBLK, NP])
        nmaxT = [sb(f"nmaxT{r}", [3 * NP, 2 * T], BF16) for r in range(2)]
        oT = sb("oT", [P, 512])
        rz = sb("rz", [P, 2 * H])
        o_tok = sb("o_tok", [P, 2, D])
        o2T = sb("o2T", [P, 2 * P])

        w_slot = [sb(f"w_slot{r}", [P, WE]) for r in range(3)]
        xs_slot = sb("xs_slot", [P, 3, D])
        xsT = sb("xsT", [P, 3, P])
        hT = sb("hT", [P, 3, NC_H, P])
        rt = hT[:, :, :, :].rearrange("p r c k -> p (r c k)").rearrange("p (c n) -> p c n", c=6)
        bias_ops = sb("bias_ops", [P, 3, 2, NC_H])
        y_slot = sb("y_slot", [P, 3, D])
        c_row = sb("c_row", [1, D])
        c_bc = sb("c_bc", [P, D])
        rb1 = sb("rb1", [P, 3, NC_H])
        y_tok = xn_all
        fin = probs[:, 0:8, :].rearrange("p (r c) n -> p r c n", r=2)

        names = """weights_in x_in0 x_in1 x_in2 x_in3 zero_src zeros_out lora_ps w_eff_done cw_in0 cw_in1 cw_in2
            crelu c_mm c_row_done c_bc_ps c_bc_done stats_done var_done std_done dve_seq ln_done
            xn_done xn_kept xT_ps xT_done qk_ps v_ps lg_ps part1_done rem_done part2_done part3_done v_done lg_done
            qk_out0 qk_out1 const_rows_in diag_zero vd_zero vd_one onehot_done rank_ps slots_done tile_expert_done scattered
            qd_ks_in0 qd_ks_in1 qs_kd_in0 qs_kd_in1 max_in0 max_in1 s_ps max_done mT_ps nmax1 nmax_r nmax2 nmax3 nmaxT_done
            vdiag_done st_ps exp_done pv_ps oT_done otok_ps rz_done otok_done o2T_ps o2T_done s_out_ps s_done
            w_in0 w_in1 w_in2 xs_in0 xs_in1 xs_in2 xsT_ps xsT_done h_ps bias1 bias_done h_done y_ps y_done
            y_out0 y_out1 y_out2 gathered fz fe fd fr fg fs fin_done out0 out1""".split()
        S = {n: sem(n) for n in names}

        def wait(eng, name, value):
            if not isinstance(value, int) or value > 0:
                eng.wait_ge(S[name], value)

        def lens(unit):
            n, pairs = UNITS[unit]
            return n, pairs, BLK * (n + 1)

        def attention_steps(body, eng):
            body(0, 0)
            with eng.Fori(0, 6) as k:
                body(k * 2 + 1, 1)
                body(k * 2 + 2, 0)
            for i in (13, 14, 15):
                body(i, i % 2)

        def has(i, low, high):
            return not isinstance(i, int) or low <= i <= high

        def expert_steps(body, eng):
            for t in range(3):
                body(t, t)
            with eng.Fori(1, SLOT_TILES // 3) as k:
                for r in range(3):
                    body(k * 3 + r, r)

        block = ctx.enter_context(nc.Block())

        @block.sync
        def _(sp):
            for c in range(4):
                for n in range(8 * c, 8 * c + 8):
                    sp.dma_start(x_all[:, n, :], x_tiles[n // 2, n % 2]).then_inc(S[f"x_in{c}"], 16)
            loads = [(cf[:, :], const_f32), (cb[:, :], const_bf16), (wp_sb[:, :], wp_t), (wr_sb[:, :], wr),
                     (br_sb[:, :], br.partition_broadcast(P)), (b2_sb[:, :], b2)]
            for n, (w, a, b) in enumerate(((wq_t, aq_t, bq), (wk_t, ak_t, bk), (wv_t, av_t, bv))):
                loads += [(w_raw[:, n, :], w), (lora_a[:, n, :], a), (lora_b[:, n, :], b)]
            assert len(loads) == 15
            for dst, src in loads:
                sp.dma_start(dst, src).then_inc(S["weights_in"], 16)
            for e in range(E):
                wait(sp, "c_mm", e - 2)
                sp.dma_start(w_slot[e % 3][:, :], w_experts[e]).then_inc(S[f"cw_in{e % 3}"], 16)
            sp.wait_ge(S["diag_zero"], 4)
            for r in range(2):
                for a in range(2):
                    rows = slice(64 * a + CONST_ROW, 64 * a + 64)
                    for dst, src in ((q_plain[r][rows], q_const_rows), (k_plain[r][rows], k_const_rows),
                                     (q_diag[r][rows, :, a], q_const_rows), (k_diag[r][rows, :, a], k_const_rows)):
                        sp.dma_start(dst, src[a].rearrange("r (p t) -> r p t", p=NP)).then_inc(S["const_rows_in"], 16)
            sp.wait_ge(S["zero_src"], 1)
            sp.dma_start(xs_dram.rearrange("(p r) d -> p (r d)", p=P),
                         probs[:, :, :].rearrange("p u c -> p (u c)")[:, 0:SLOT_TILES * D]).then_inc(S["zeros_out"], 16)

            def store_parts(b, r):
                sp.wait_ge(S["part3_done"], b + 1)
                sp.dma_start(qk_dram[bass.ds(b, 1)].rearrange("o c s p t -> p (o c s) t"),
                             parts[:, r].rearrange("p c s t -> p (c s) t")).then_inc(S[f"qk_out{r}"], 16)
            with sp.Fori(0, NB // 2) as k:
                for r in range(2):
                    store_parts(k * 2 + r, r)
            sp.wait_ge(S["qk_out0"], 16 * NB // 2)
            sp.wait_ge(S["qk_out1"], 16 * NB // 2)
            sp.wait_ge(S["const_rows_in"], 16 * 16)

            def load_stack(dst, diag, is_q, b, name):
                for a in range(2):
                    row = 64 * a
                    for (part, copies), kparts in zip(TERMS_Q, TERMS_K):
                        src = qk_dram[bass.ds(b, 1), :, 0 if is_q else 1, 64 * a:64 * a + 64]
                        if diag:
                            for c in range(copies):
                                which = part if is_q else kparts[c]
                                sp.dma_start(dst[row:row + DH, :, a],
                                             src[:, which:which + 1].rearrange("o c (d p) t -> (o c d) p t", p=NP)).then_inc(S[name], 16)
                                row += DH
                            continue
                        if is_q:
                            src = src[:, part:part + 1].rearrange("o c (d p) t -> (o c) d (p t)", p=NP).to_broadcast([copies, DH, NP * T])
                        else:
                            src = src[:, 0:copies].rearrange("o c (d p) t -> (o c) d (p t)", p=NP)
                        sp.dma_start(dst[row:row + copies * DH].rearrange("r p t -> r (p t)"), src).then_inc(S[name], 16)
                        row += copies * DH

            def load_for_max(b, r):
                load_stack(q_diag[r], True, True, b, f"qd_ks_in{r}")
                load_stack(k_plain[r], False, False, b, f"qd_ks_in{r}")

            def load_for_probs(b, r):
                load_stack(q_plain[r], False, True, b, f"qs_kd_in{r}")
                load_stack(k_diag[r], True, False, b, f"qs_kd_in{r}")

            def load_max_rows(b, r):
                sp.wait_ge(S["nmaxT_done"], b + 1)
                for a in range(2):
                    for c in range(3):
                        row = 64 * a + MAX_ROW + c
                        sp.dma_start(q_plain[r][row:row + 1],
                                     nmaxT[r][NP * c:NP * c + NP, a * T:(a + 1) * T]).then_inc(S[f"max_in{r}"], 16)

            load_for_max(0, 0)
            load_for_max(1, 1)
            load_for_probs(0, 0)
            sp.wait_ge(S["s_ps"], NU)
            load_for_max(2, 0)
            load_max_rows(0, 0)

            def step(i, r):
                if has(i, 0, 14):
                    wait(sp, "st_ps", i * NU)
                    load_for_probs(i + 1, 1 - r)
                if has(i, 0, 12):
                    sp.wait_ge(S["s_ps"], (i + 2) * NU)
                    load_for_max(i + 3, 1 - r)
                if has(i, 0, 14):
                    load_max_rows(i + 1, 1 - r)
            attention_steps(step, sp)

            sp.wait_ge(S["tile_expert_done"], 1)
            sp.wait_ge(S["scattered"], 16 * NT)

            def tile(t, r):
                wait(sp, "y_ps", t - 2)
                e = sp.value_load(tile_expert[0:1, bass.ds(t, 1)], min_val=0, max_val=E - 1)
                sp.dma_start(w_slot[r][:, :], w_experts[bass.ds(e, 1)].rearrange("o p f -> (o p) f")).then_inc(S[f"w_in{r}"], 16)
                sp.dma_start(xs_slot[:, r, :], xs_dram[bass.ds(t * P, P), :]).then_inc(S[f"xs_in{r}"], 16)
            expert_steps(tile, sp)

            for c in range(8):
                sp.wait_ge(S["fin_done"], c + 1)
                for n in range(4):
                    sp.dma_start(out_tiles[2 * c + n // 2, n % 2],
                                 fin[:, c % 2, 3, n * D:(n + 1) * D]).then_inc(S[f"out{c % 2}"], 16)
            sp.wait_ge(S["out0"], 4 * 4 * 16)
            sp.wait_ge(S["out1"], 4 * 4 * 16)

        @block.gpsimd
        def _(pool):
            pool.memset(probs[:, :, :], 0.0).then_inc(S["zero_src"], 1)
            for r in range(2):
                pool.memset(q_diag[r][:, :, :, :], 0.0).then_inc(S["diag_zero"], 1)
                pool.memset(k_diag[r][:, :, :, :], 0.0).then_inc(S["diag_zero"], 1)
                pool.memset(v_diag[r][:, :, :, :], 0.0).then_inc(S["vd_zero"], 1)
            pool.wait_ge(S["vd_zero"], 2)
            pool.wait_ge(S["weights_in"], 16 * 15)
            for r in range(2):
                pool.tensor_copy(v_halves[r][:, :, :, DH], of_half.unsqueeze(1).to_broadcast([P, NBLK * NP, 2])).then_inc(S["vd_one"], 1)
            pool.wait_ge(S["vd_one"], 2)

            def split(b, r):
                pool.wait_ge(S["xn_done"], 2 * b + 2)
                pool.wait_ge(S["vd_one"], 2)
                pool.tensor_copy(xn_all[:, bass.ds(b * 2, 2), :], xn_slot[:, r]).then_inc(S["xn_kept"], 1)
                pool.wait_ge(S["part2_done"], b + 1)
                pool.tensor_tensor(parts[:, r, 2], rem[:, r].rearrange("p (s t) -> p s t", s=2), parts[:, r, 1], ALU.subtract).then_inc(S["part3_done"], 1)
            for r in range(2):
                split(r, r)
            with pool.Fori(1, NB // 2) as k:
                for r in range(2):
                    pool.wait_ge(S[f"qk_out{r}"], k * 16)
                    split(k * 2 + r, r)

            def spread_v(b, r):
                v = v_all[:, bass.ds(b, 1)].rearrange("p o n h d -> p (o n h) d")
                pool.tensor_tensor(v_halves[r][:, :, :, 0:DH], v.unsqueeze(2).to_broadcast([P, NBLK * NP, 2, DH]),
                                   of_half.unsqueeze(1).unsqueeze(3).to_broadcast([P, NBLK * NP, 2, DH]),
                                   ALU.mult).then_inc(S["vdiag_done"], 1)
            pool.wait_ge(S["v_done"], NB)
            spread_v(0, 0)

            pool.wait_ge(S["slots_done"], 1)
            pool.wait_ge(S["zeros_out"], 16)
            pool.wait_ge(S["xn_kept"], NB)
            for n in range(NT):
                pool.indirect_dma_start(xs_dram[:, :], bass.IndirectOffsetOnAxis(slot_of[:, n:n + 1], axis=0),
                                        xn_all[:, n, :], None).then_inc(S["scattered"], 16)

            def step(i, r):
                if has(i, 0, 14):
                    wait(pool, "pv_ps", i * NPV)
                    spread_v(i + 1, 1 - r)
            attention_steps(step, pool)

            for r in range(3):
                pool.wait_ge(S[f"y_out{r}"], 16 * SLOT_TILES // 3)
            for n in range(NT):
                pool.indirect_dma_start(y_tok[:, n, :], None, y_dram[:, :],
                                        bass.IndirectOffsetOnAxis(slot_of[:, n:n + 1], axis=0)).then_inc(S["gathered"], 16)

        @block.scalar
        def _(act):
            act.wait_ge(S["var_done"], 1)
            act.activation(ln[:, 4, :], ln[:, 3, :], ACT.Sqrt).then_inc(S["std_done"], 1)
            for e in range(E):
                act.wait_ge(S[f"cw_in{e % 3}"], 16 * (e // 3 + 1))
                wait(act, "c_mm", e - 2)
                act.activation(rb1[:, e % 3, :], w_slot[e % 3][:, HID + NC_H * D:WE], ACT.Relu).then_inc(S["crelu"], 1)
            act.wait_ge(S["c_mm"], E + 1)
            act.activation(c_row[:, :], bank[6][0:1, 0:D], ACT.Copy).then_inc(S["c_row_done"], 1)
            act.wait_ge(S["c_bc_ps"], 1)
            act.activation(c_bc[:, :], bank[7][:, 0:D], ACT.Copy).then_inc(S["c_bc_done"], 1)

            def evacuate(b, r, first):
                act.wait_ge(S["xT_ps"], b + 1)
                if not first:
                    act.wait_ge(S["lg_ps"], b - 1)
                act.activation(xnT_slot[:, r, :], bank[r][:, 0:T], ACT.Copy).then_inc(S["xT_done"], 1)
                act.wait_ge(S["qk_ps"], b + 1)
                if not first:
                    act.wait_ge(S[f"qk_out{r}"], (b - r) * 8)
                act.activation(parts[:, r, 0], bank[2 + r][:, :].rearrange("p (s t) -> p s t", s=2), ACT.Copy).then_inc(S["part1_done"], 1)
                act.wait_ge(S["v_ps"], b + 1)
                act.activation(v_all[:, bass.ds(b, 1)].rearrange("p o n h d -> p (o n h d)"),
                               bank[4 + r][:, 0:T], ACT.Copy).then_inc(S["v_done"], 1)
                act.wait_ge(S["rem_done"], b + 1)
                act.activation(parts[:, r, 1], rem[:, r].rearrange("p (s t) -> p s t", s=2), ACT.Copy).then_inc(S["part2_done"], 1)
            for r in range(2):
                evacuate(r, r, True)
            with act.Fori(1, NB // 2) as k:
                for r in range(2):
                    evacuate(k * 2 + r, r, False)

            def max_rows(b, r):
                act.wait_ge(S["mT_ps"], b + 1)
                if has(b, 2, 15):
                    act.wait_ge(S[f"max_in{r}"], (b - r) * 48)
                act.activation(nmaxT[r][:, :], bank[5][0:3 * NP, :], ACT.Copy).then_inc(S["nmaxT_done"], 1)

            def out_o2T(b):
                act.wait_ge(S["o2T_ps"], b + 1)
                act.activation(o2T[:, :], bank[7][:, 0:2 * P], ACT.Copy).then_inc(S["o2T_done"], 1)

            def out_s(b):
                act.wait_ge(S["s_out_ps"], b + 1)
                act.activation(s_all[:, bass.ds(b * 2, 2), :], bank[7][:, 2 * P:4 * P].rearrange("p (j d) -> p j d", d=D),
                               ACT.Copy).then_inc(S["s_done"], 1)

            max_rows(0, 0)

            def step(i, r):
                if has(i, 0, 14):
                    max_rows(i + 1, 1 - r)
                for u in range(NU):
                    n, pairs, ln_u = lens(u)
                    w = ln_u * len(pairs)
                    act.wait_ge(S["st_ps"], i * NU + u + 1)
                    wait(act, "pv_ps", i * NPV)
                    act.activation(probs[:, u, 0:w], bank[2 + (u + r) % 2][:, 0:w], ACT.Exp).then_inc(S["exp_done"], 1)
                    if has(i, 1, 15):
                        if u == 5:
                            out_o2T(i - 1)
                        if u == 8:
                            out_s(i - 1)
                act.wait_ge(S["pv_ps"], (i + 1) * NPV)
                wait(act, "otok_ps", i)
                act.activation(oT[:, :], bank[4][:, :], ACT.Copy).then_inc(S["oT_done"], 1)
            attention_steps(step, act)
            out_o2T(NB - 1)
            out_s(NB - 1)

            def evac_x(t, r):
                act.wait_ge(S["xsT_ps"], t + 1)
                wait(act, "h_ps", t - 2)
                act.activation(xsT[:, r, :], bank[0][:, 0:P], ACT.Copy).then_inc(S["xsT_done"], 1)

            def store_y(t, r, first):
                act.wait_ge(S["y_ps"], t + 1)
                if not first:
                    act.wait_ge(S[f"y_out{r}"], (t - r) // 3 * 16 if isinstance(t, int) else t_count[0])
                act.activation(y_slot[:, r, :], bank[4 + r][:, 0:D], ACT.Copy).then_inc(S["y_done"], 1)
                act.wait_ge(S["y_done"], t + 1)
                act.dma_start(y_dram[bass.ds(t * P, P), :], y_slot[:, r, :]).then_inc(S[f"y_out{r}"], 16)
            t_count = [None]
            for t in range(3):
                evac_x(t, t)
                store_y(t, t, True)
            with act.Fori(1, SLOT_TILES // 3) as k:
                for r in range(3):
                    t_count[0] = k * 16
                    evac_x(k * 3 + r, r)
                    store_y(k * 3 + r, r, False)

            for c in range(8):
                act.wait_ge(S["fz"], c + 1)
                act.activation(fin[:, c % 2, 1, :], fin[:, c % 2, 0, :], ACT.Exp, scale=-1.0).then_inc(S["fe"], 1)

        @block.vector
        def _(dve):
            seq = [0]

            def then(ins):
                seq[0] += 1
                ins.then_inc(S["dve_seq"], 1)
                dve.wait_ge(S["dve_seq"], seq[0])

            for c in range(4):
                dve.wait_ge(S[f"x_in{c}"], 8 * 16)
                for n in range(8 * c, 8 * c + 8):
                    last = dve.bn_stats(stats[:, n, :], x_all[:, n, :])
            then(last)
            mean_e, m2_e, mean_o, m2_o = (stats[:, :, c] for c in (1, 2, 4, 5))
            dve.tensor_tensor(ln[:, 0, :], mean_e, mean_o, ALU.add)
            dve.tensor_tensor(ln[:, 1, :], mean_e, mean_o, ALU.subtract)
            then(dve.tensor_tensor(ln[:, 2, :], m2_e, m2_o, ALU.add))
            then(dve.tensor_tensor(ln[:, 1, :], ln[:, 1, :], ln[:, 1, :], ALU.mult))
            then(dve.tensor_scalar(ln[:, 2, :], ln[:, 2, :], 1.0 / D, EPS, ALU.mult, ALU.add))
            dve.scalar_tensor_tensor(ln[:, 3, :], ln[:, 1, :], 0.25, ln[:, 2, :], ALU.mult, ALU.add).then_inc(S["var_done"], 1)
            dve.wait_ge(S["std_done"], 1)
            then(dve.reciprocal(ln[:, 5, :], ln[:, 4, :]))
            then(dve.tensor_tensor(ln[:, 6, :], ln[:, 5, :], ln[:, 5, :], ALU.mult))
            then(dve.tensor_tensor(ln[:, 6, :], ln[:, 6, :], ln[:, 3, :], ALU.mult))
            then(dve.tensor_scalar(ln[:, 6, :], ln[:, 6, :], -0.5, 1.5, ALU.mult, ALU.add))
            then(dve.tensor_tensor(rstd[:, :], ln[:, 5, :], ln[:, 6, :], ALU.mult))
            then(dve.scalar_tensor_tensor(nmr[:, :], ln[:, 0, :], -0.5, rstd[:, :], ALU.mult, ALU.mult))

            dve.wait_ge(S["lora_ps"], 1)
            for n in range(3):
                last = dve.scalar_tensor_tensor(w_eff[:, n, :], bank[0][:, n * P:(n + 1) * P], LORA_SCALE, w_raw[:, n, :],
                                                ALU.mult, ALU.add)
            then(last)
            dve.tensor_scalar(w_eff[:, 0, :], w_eff[:, 0, :], float(DH) ** -0.5, None, ALU.mult).then_inc(S["w_eff_done"], 1)

            def normalise(b, r, first):
                if not first:
                    dve.wait_ge(S["xT_ps"], b - 1)
                    dve.wait_ge(S["xn_kept"], b - 1)
                for j in range(2):
                    tile = bass.ds(b * 2 + j, 1)
                    dve.tensor_scalar(xn_slot[:, r, j, :], x_all[:, tile, :].rearrange("p o d -> p (o d)"),
                                      rstd[:, tile], nmr[:, tile], ALU.mult, ALU.add).then_inc(S["xn_done"], 1)

            def remainder(b, r, first):
                dve.wait_ge(S["part1_done"], b + 1)
                if not first:
                    dve.wait_ge(S["part3_done"], b - 1)
                dve.tensor_tensor(rem[:, r].rearrange("p (s t) -> p s t", s=2), bank[2 + r][:, :].rearrange("p (s t) -> p s t", s=2),
                                  parts[:, r, 0], ALU.subtract).then_inc(S["rem_done"], 1)
                dve.wait_ge(S["lg_ps"], b + 1)
                dve.tensor_tensor(logits[:, bass.ds(b * 2, 2), :], bank[6 + r][:, 0:2 * E].rearrange("p (j e) -> p j e", e=E),
                                  br_sb[:, :].unsqueeze(1).to_broadcast([P, 2, E]), ALU.add).then_inc(S["lg_done"], 1)
            normalise(0, 0, True)
            normalise(1, 1, True)
            remainder(0, 0, True)
            normalise(2, 0, False)
            remainder(1, 1, True)
            with dve.Fori(0, NB // 2 - 2) as k:
                normalise(k * 2 + 3, 1, False)
                remainder(k * 2 + 2, 0, False)
                normalise(k * 2 + 4, 0, False)
                remainder(k * 2 + 3, 1, False)
            normalise(NB - 1, 1, False)
            remainder(NB - 2, 0, False)
            remainder(NB - 1, 1, False)

            dve.wait_ge(S["lg_done"], NB)
            lg = logits[:, :, :]
            shape = [P, NT, E]
            m3 = [rt[:, c, :].rearrange("p (n e) -> p n e", e=E) for c in range(6)]
            iota3 = iota8.unsqueeze(1).to_broadcast(shape)
            then(dve.tensor_reduce(r32[:, 0, :], lg, AX.X, ALU.max))
            then(dve.tensor_tensor(m3[0], lg, r32[:, 0, :].unsqueeze(2).to_broadcast(shape), ALU.is_equal))
            then(dve.scalar_tensor_tensor(m3[1], m3[0], -float(E), iota3, ALU.mult, ALU.add))
            then(dve.tensor_reduce(r32[:, 1, :], m3[1], AX.X, ALU.min))
            then(dve.tensor_scalar(r32[:, 1, :], r32[:, 1, :], float(E), None, ALU.add))
            then(dve.tensor_tensor(m3[0], iota3, r32[:, 1, :].unsqueeze(2).to_broadcast(shape), ALU.is_equal))
            dve.tensor_copy(onehot_b[:, :, :], m3[0]).then_inc(S["onehot_done"], 1)
            dve.wait_ge(S["rank_ps"], 2)
            dve.memset(r32[:, 2, :], 0.0)
            then(dve.tensor_copy(m3[1], bank[7][:, 0:NT * E].rearrange("p (n e) -> p n e", e=E)))
            for e in range(E):
                last = dve.tensor_tensor_scan(m3[2][:, :, e], m3[1][:, :, e], r32[:, 2, :], 0.0, ALU.add, ALU.add)
            then(last)
            then(dve.tensor_scalar(r8[:, 0, :], m3[2][:, NT - 1, :], float(P - 1), None, ALU.add))
            then(dve.tensor_copy(r8i[:, 0, :], r8[:, 0, :]))
            then(dve.tensor_scalar(r8i[:, 1, :], r8i[:, 0, :], P.bit_length() - 1, None, ALU.arith_shift_right))
            then(dve.tensor_copy(r8[:, 1, :], r8i[:, 1, :]))
            then(dve.tensor_tensor_scan(r8[:, 2, :], r8[:, 1, :], r32[:, 2, 0:E], 0.0, ALU.add, ALU.add))
            then(dve.tensor_tensor(r8[:, 3, :], r8[:, 2, :], r8[:, 1, :], ALU.subtract))
            then(dve.tensor_scalar(r8[:, 4, :], r8[:, 3, :], float(P), None, ALU.mult))
            then(dve.tensor_tensor(m3[3], m3[2], m3[1], ALU.subtract))
            then(dve.tensor_tensor(m3[4], bank[6][:, 0:NT * E].rearrange("p (n e) -> p n e", e=E), m3[3], ALU.add))
            then(dve.tensor_tensor(m3[5], m3[4], r8[:, 4, :].unsqueeze(1).to_broadcast(shape), ALU.add))
            then(dve.tensor_tensor(m3[4], m3[5], m3[0], ALU.mult))
            then(dve.tensor_reduce(r32[:, 3, :], m3[4], AX.X, ALU.add))
            dve.tensor_copy(slot_of[:, :], r32[:, 3, :]).then_inc(S["slots_done"], 1)
            te_shape = [1, SLOT_TILES, E]
            then(dve.tensor_tensor(te_cmp[:, :, :], iota_tile.unsqueeze(2).to_broadcast(te_shape),
                                   r8[0:1, 2, :].unsqueeze(1).to_broadcast(te_shape), ALU.is_ge))
            then(dve.tensor_reduce(te_f[:, 0, :], te_cmp[:, :, :], AX.X, ALU.add))
            then(dve.tensor_scalar(te_f[:, 1, :], te_f[:, 0, :], float(E - 1), None, ALU.min))
            dve.tensor_copy(tile_expert[:, :], te_f[:, 1, :]).then_inc(S["tile_expert_done"], 1)

            def unit_max(b, r, u):
                n, pairs, ln_u = lens(u)
                dve.wait_ge(S["s_ps"], b * NU + u + 1)
                dve.tensor_reduce(row_max[r][:, n, pairs[0]:pairs[-1] + 1],
                                  bank[(u + r) % 2][:, 0:ln_u * len(pairs)].rearrange("p (c k) -> p c k", k=ln_u),
                                  AX.X, ALU.max).then_inc(S["max_done"], 1)

            def max_parts(b, r):
                dve.wait_ge(S["max_done"], (b + 1) * NU)
                if has(b, 2, 15):
                    dve.wait_ge(S["mT_ps"], b - 1)
                dve.tensor_scalar(nmax[r][:, :, 0, :], row_max[r][:, :, :], -1.0, None, ALU.mult).then_inc(S["nmax1"], 1)
                dve.wait_ge(S["nmax1"], b + 1)
                dve.scalar_tensor_tensor(nmax_rem[:, :, :], row_max[r][:, :, :], -1.0, nmax[r][:, :, 0, :],
                                         ALU.mult, ALU.subtract).then_inc(S["nmax_r"], 1)
                dve.wait_ge(S["nmax_r"], b + 1)
                dve.tensor_copy(nmax[r][:, :, 1, :], nmax_rem[:, :, :]).then_inc(S["nmax2"], 1)
                dve.wait_ge(S["nmax2"], b + 1)
                dve.tensor_tensor(nmax[r][:, :, 2, :], nmax_rem[:, :, :], nmax[r][:, :, 1, :], ALU.subtract).then_inc(S["nmax3"], 1)

            def divide(b):
                dve.wait_ge(S["otok_ps"], b + 1)
                ov = bank[6][:, :].rearrange("p (c k) -> p c k", k=16)
                wait(dve, "o2T_ps", b)
                dve.reciprocal(rz[:, :], ov[:, :, DH]).then_inc(S["rz_done"], 1)
                dve.wait_ge(S["rz_done"], b + 1)
                dve.tensor_tensor(o_tok[:, :, :].rearrange("p j (c d) -> p (j c) d", d=DH), ov[:, :, 0:DH],
                                  rz[:, :].unsqueeze(2).to_broadcast([P, 2 * H, DH]), ALU.mult).then_inc(S["otok_done"], 1)

            for b in range(2):
                for u in range(NU):
                    unit_max(b, b, u)
                max_parts(b, b)

            def step(i, r):
                for u in range(NU):
                    if has(i, 0, 13):
                        unit_max(i + 2, r, u)
                    if u == 1 and has(i, 1, 15):
                        divide(i - 1)
                if has(i, 0, 13):
                    max_parts(i + 2, r)
            attention_steps(step, dve)
            divide(NB - 1)

            def relu(t, r):
                dve.wait_ge(S["h_ps"], t + 1)
                wait(dve, "y_ps", t - 2)
                b1 = w_slot[r][:, HID + NC_H * D:WE]
                dve.tensor_scalar(bias_ops[:, r, 0, :], b1, -1.0, None, ALU.mult).then_inc(S["bias1"], 1)
                dve.tensor_scalar(bias_ops[:, r, 1, :], b1, 0.0, None, ALU.min).then_inc(S["bias1"], 1)
                dve.wait_ge(S["bias1"], t * 2 + 2)
                for c in range(NC_H):
                    last = dve.tensor_scalar(hT[:, r, c, :], bank[1 + r][:, c * P:(c + 1) * P], bias_ops[:, r, 0, c:c + 1],
                                             bias_ops[:, r, 1, c:c + 1], ALU.max, ALU.add)
                last.then_inc(S["h_done"], 1)
            expert_steps(relu, dve)

            dve.wait_ge(S["c_bc_done"], 1)
            dve.wait_ge(S["s_done"], NB)
            for c in range(8):
                z, ez, g, o = (fin[:, c % 2, n, :] for n in range(4))
                tiles = slice(4 * c, 4 * c + 4)
                dve.wait_ge(S["gathered"], 16 * NT)
                dve.tensor_tensor(z.rearrange("p (j d) -> p j d", d=D), y_tok[:, tiles, :],
                                  c_bc[:, :].unsqueeze(1).to_broadcast([P, 4, D]), ALU.add).then_inc(S["fz"], 1)
                dve.wait_ge(S["fe"], c + 1)
                then(dve.tensor_scalar(ez, ez, 1.0, None, ALU.add))
                then(dve.reciprocal(g, ez))
                then(dve.tensor_tensor(g, g, z, ALU.mult))
                then(dve.tensor_tensor(g.rearrange("p (j d) -> p j d", d=D), g.rearrange("p (j d) -> p j d", d=D),
                                       s_all[:, tiles, :], ALU.mult))
                wait(dve, f"out{c % 2}", 4 * 16 * (c // 2))
                dve.tensor_tensor(o.rearrange("p (j d) -> p j d", d=D), g.rearrange("p (j d) -> p j d", d=D),
                                  x_all[:, tiles, :], ALU.add).then_inc(S["fin_done"], 1)

        @block.tensor
        def _(pe):
            pe.wait_ge(S["weights_in"], 16 * 15)
            for n in range(3):
                last = pe.matmul(bank[0][:, n * P:(n + 1) * P], lora_b[:, n, :], lora_a[:, n, :], start=(n == 0), stop=True,
                                 skip_group_check=True)
            last.then_inc(S["lora_ps"], 1)
            for e in range(E):
                pe.wait_ge(S["crelu"], e + 1)
                for c in range(NC_H):
                    last = pe.matmul(bank[6][0:1, 0:D], rb1[:, e % 3, c:c + 1],
                                     w_slot[e % 3][:, HID + c * D:HID + (c + 1) * D], start=(e == 0 and c == 0), stop=False)
                last.then_inc(S["c_mm"], 1)
            pe.matmul(bank[6][0:1, 0:D], ones_f[0:E, 0:1], b2_sb[:, :], start=False, stop=True).then_inc(S["c_mm"], 1)
            pe.wait_ge(S["c_row_done"], 1)
            pe.matmul(bank[7][:, 0:D], ones_f[0:1, :], c_row[:, :], start=True, stop=True).then_inc(S["c_bc_ps"], 1)
            pe.wait_ge(S["w_eff_done"], 1)
            pe.wait_ge(S["c_bc_done"], 1)

            def project(b, r, first):
                pe.wait_ge(S["xn_done"], 2 * b + 2)
                if not first:
                    pe.wait_ge(S["xT_done"], b - 1)
                for j in range(2):
                    last = pe.transpose(bank[r][:, j * P:(j + 1) * P], xn_slot[:, r, j, :], ident_f)
                last.then_inc(S["xT_ps"], 1)
                pe.wait_ge(S["xT_done"], b + 1)
                if not first:
                    pe.wait_ge(S["rem_done"], b - 1)
                for n in range(2):
                    last = pe.matmul(bank[2 + r][:, n * T:(n + 1) * T], w_eff[:, n, :], xnT_slot[:, r, :], start=(n == 0),
                                     stop=True, skip_group_check=True)
                last.then_inc(S["qk_ps"], 1)
                if not first:
                    pe.wait_ge(S["v_done"], b - 1)
                for n in range(NBLK):
                    for a in range(2):
                        last = pe.matmul(bank[4 + r][64 * a:64 * a + 64, n * BLK:(n + 1) * BLK], xnT_slot[:, r, n::NBLK],
                                         w_eff[:, 2, 64 * a:64 * a + 64], start=(n == 0), stop=True, skip_group_check=True)
                last.then_inc(S["v_ps"], 1)
                if not first:
                    pe.wait_ge(S["lg_done"], b - 1)
                for j in range(2):
                    last = pe.matmul(bank[6 + r][:, j * E:(j + 1) * E], xnT_slot[:, r, j * P:(j + 1) * P], wr_sb[:, :],
                                     start=(j == 0), stop=True, skip_group_check=True)
                last.then_inc(S["lg_ps"], 1)
            for r in range(2):
                project(r, r, True)
            with pe.Fori(1, NB // 2) as k:
                for r in range(2):
                    project(k * 2 + r, r, False)

            pe.wait_ge(S["onehot_done"], 1)
            oh = onehot_b[:, :, :].rearrange("p n e -> p (n e)")
            pe.matmul(bank[6][:, 0:NT * E], before_b, oh, start=True, stop=True).then_inc(S["rank_ps"], 1)
            pe.matmul(bank[7][:, 0:NT * E], ones_b, oh, start=True, stop=True).then_inc(S["rank_ps"], 1)

            def blocks(columns, low, high):
                return columns.rearrange("p (i k) -> p i k", k=NBLK)[:, :, low:high]

            def max_scores(b, r, u):
                n, pairs, ln_u = lens(u)
                if u == 0:
                    pe.wait_ge(S[f"qd_ks_in{r}"], (b - r) * (LOADS * 8) + LOADS * 16)
                wait(pe, "max_done", b * NU + u - 1)
                ps = bank[(u + r) % 2]
                for c, p in enumerate(pairs):
                    pe.matmul(ps[:, c * ln_u:(c + 1) * ln_u], q_diag[r][:, p].rearrange("x h t -> x (h t)")[:, n::NBLK], blocks(k_plain[r][:, p, :], 0, n + 1),
                              start=(c == 0), stop=False, skip_group_check=True)
                pe.matmul(ps[:, 0:ln_u * len(pairs)].rearrange("p (c k) -> p c k", k=ln_u)[:, :, n::n + 1], ident_b,
                          mask_qk.unsqueeze(1).to_broadcast([P, len(pairs), BLK]), start=False, stop=True,
                          skip_group_check=True).then_inc(S["s_ps"], 1)

            def scores(b, r, u):
                n, pairs, ln_u = lens(u)
                kb = NBLK - 1 - n
                if u == 0:
                    pe.wait_ge(S[f"qs_kd_in{r}"], (b - r) * (LOADS * 8) + LOADS * 16)
                    pe.wait_ge(S[f"max_in{r}"], (b - r) * 48 + 96)
                wait(pe, "exp_done", b * NU + u - 1)
                ps = bank[2 + (u + r) % 2]
                for c, p in enumerate(pairs):
                    pe.matmul(ps[:, c * ln_u:(c + 1) * ln_u], k_diag[r][:, p].rearrange("x h t -> x (h t)")[:, kb::NBLK], blocks(q_plain[r][:, p, :], kb, NBLK),
                              start=(c == 0), stop=False, skip_group_check=True)
                pe.matmul(ps[:, 0:ln_u * len(pairs)].rearrange("p (c k) -> p c k", k=ln_u)[:, :, 0::n + 1], ident_b,
                          mask_kq.unsqueeze(1).to_broadcast([P, len(pairs), BLK]), start=False, stop=True,
                          skip_group_check=True).then_inc(S["st_ps"], 1)

            def values(b, r, u):
                if u == 1:
                    pe.wait_ge(S["vdiag_done"], b + 1)
                    wait(pe, "oT_done", b)
                pe.wait_ge(S["exp_done"], b * NU + u + 1)
                for w in PV_AFTER[u]:
                    n, pairs, ln_u = lens(w)
                    kb = NBLK - 1 - n
                    for c, p in enumerate(pairs):
                        j, g = p % 4, p // 4
                        last = pe.matmul(blocks(bank[4][32 * j:32 * j + 32, g * T:(g + 1) * T], kb, NBLK), v_diag[r][:, kb, p, :],
                                         probs[:, w, c * ln_u:(c + 1) * ln_u], start=(kb == 0 and g == 0), stop=(kb == NBLK - 1),
                                         skip_group_check=True)
                last.then_inc(S["pv_ps"], 1)

            def turn_max(b, r):
                pe.wait_ge(S["nmax3"], b + 1)
                wait(pe, "nmaxT_done", b)
                for n in range(NBLK):
                    last = pe.matmul(bank[5][0:3 * NP, n::NBLK], nmax[r][:, n].rearrange("p c h -> p (c h)"), ident_b, start=(n == 0),
                                     stop=True, skip_group_check=True)
                last.then_inc(S["mT_ps"], 1)

            def turn_o(b):
                pe.wait_ge(S["oT_done"], b + 1)
                wait(pe, "otok_done", b)
                for j in range(2):
                    for g in range(2):
                        last = pe.transpose(bank[6][:, (j * 2 + g) * P:(j * 2 + g + 1) * P], oT[:, g * T + j * P:g * T + (j + 1) * P], ident_f)
                last.then_inc(S["otok_ps"], 1)

            def turn_o_back(b):
                pe.wait_ge(S["otok_done"], b + 1)
                wait(pe, "s_done", b)
                for j in range(2):
                    last = pe.transpose(bank[7][:, j * P:(j + 1) * P], o_tok[:, j, :], ident_f)
                last.then_inc(S["o2T_ps"], 1)

            def out_project(b):
                pe.wait_ge(S["o2T_done"], b + 1)
                for j in range(2):
                    last = pe.matmul(bank[7][:, (2 + j) * P:(3 + j) * P], o2T[:, j * P:(j + 1) * P], wp_sb[:, :],
                                     start=True, stop=True, skip_group_check=True)
                last.then_inc(S["s_out_ps"], 1)

            pe.wait_ge(S["part3_done"], NB)
            pe.wait_ge(S["slots_done"], 1)
            for b in range(2):
                for u in range(NU):
                    max_scores(b, b, u)
            turn_max(0, 0)

            def step(i, r):
                if has(i, 0, 14):
                    turn_max(i + 1, 1 - r)
                if has(i, 1, 15):
                    turn_o(i - 1)
                for u in range(NU):
                    scores(i, r, u)
                    if has(i, 0, 13):
                        max_scores(i + 2, r, u)
                    if u - 1 in PV_AFTER:
                        values(i, r, u - 1)
                    if has(i, 1, 15):
                        if u == 4:
                            turn_o_back(i - 1)
                        if u == 7:
                            out_project(i - 1)
                values(i, r, NU - 1)
            attention_steps(step, pe)
            turn_o(NB - 1)
            turn_o_back(NB - 1)
            out_project(NB - 1)

            def tile(t, r):
                pe.wait_ge(S[f"xs_in{r}"], xs_count(t, r))
                wait(pe, "xsT_done", t)
                pe.transpose(bank[0][:, 0:P], xs_slot[:, r, :], ident_f).then_inc(S["xsT_ps"], 1)
                pe.wait_ge(S["xsT_done"], t + 1)
                pe.wait_ge(S[f"w_in{r}"], xs_count(t, r))
                wait(pe, "h_done", t - 2)
                for c in range(NC_H):
                    last = pe.matmul(bank[1 + r][:, c * P:(c + 1) * P], w_slot[r][:, c * P:(c + 1) * P], xsT[:, r, :], start=(c == 0),
                                     stop=True, skip_group_check=True)
                last.then_inc(S["h_ps"], 1)
                pe.wait_ge(S["h_done"], t + 1)
                wait(pe, "y_done", t - 2)
                for c in range(NC_H):
                    last = pe.matmul(bank[4 + r][:, 0:D], hT[:, r, c, :], w_slot[r][:, HID + c * D:HID + (c + 1) * D],
                                     start=(c == 0), stop=(c == NC_H - 1))
                last.then_inc(S["y_ps"], 1)
            pe.wait_ge(S["s_done"], NB)
            turn = [None]

            def xs_count(t, r):
                return 16 if isinstance(t, int) else turn[0] * 16 + 16
            for t in range(3):
                tile(t, t)
            with pe.Fori(1, SLOT_TILES // 3) as k:
                turn[0] = k
                for r in range(3):
                    tile(k * 3 + r, r)


def shape_constants():
    def bf16_bits(a):
        u = np.asarray(a, np.float32).view(np.uint32)
        return ((u + 0x7fff + ((u >> 16) & 1)) >> 16).astype(np.uint16)

    def value(bits):
        return (bits.astype(np.uint32) << 16).view(np.float32)

    f = np.zeros((P, 2 * P + 64), np.float32)
    f[:, 0:P] = np.eye(P)
    f[:, P:2 * P] = 1.0
    f[:, 2 * P:2 * P + 8] = np.arange(8)
    f[:, 2 * P + 8:2 * P + 8 + SLOT_TILES] = np.arange(SLOT_TILES)
    f[0:BLK, 2 * P + 50] = 1
    f[BLK:, 2 * P + 51] = 1
    i, j = np.arange(P)[:, None] % BLK, np.arange(BLK)[None, :]
    n, m = np.arange(P)[:, None], np.arange(P)[None, :]
    b = np.concatenate([np.where(j > i, NEG, 0), np.where(j < i, NEG, 0), n == m, n < m, np.ones((P, P))], axis=1)
    start = 2.0 ** (-2.0 ** (-(np.log2(H) - 3)))
    slope = np.array([start * start ** h for h in range(H)], np.float32).astype(np.float64)
    rise = slope.reshape(NP, 2).T[:, :, None] * (np.arange(T) % NBLK * BLK + np.arange(T) // NBLK)
    rise = rise.reshape(2, NP * T)
    cut, rest = [], rise
    for _ in range(3):
        cut.append(value(bf16_bits(rest)))
        rest = rest - cut[-1].astype(np.float64)
    q, k = np.zeros((2, 16, NP * T)), np.zeros((2, 16, NP * T))
    for c in range(3):
        q[:, c], k[:, c] = 1, -cut[c]
        q[:, 3 + c], k[:, 3 + c] = cut[c], 1
        k[:, 6 + c] = 1
    return f, bf16_bits(b), bf16_bits(q), bf16_bits(k)


def kernel(L0_attn_x, L0_attn_Wq, L0_attn_Aq, L0_attn_Bq, L0_attn_Wk, L0_attn_Ak, L0_attn_Bk, L0_attn_Wv, L0_attn_Av,
           L0_attn_Bv, L0_attn_Wp, L0_ffn_W1, L0_ffn_b1, L0_ffn_W2, L0_ffn_b2, L0_ffn_Wr, L0_ffn_br):
    import concourse.bacc as bacc
    from concourse.bass_utils import run_bass_kernel_spmd

    def pair_order(w):
        w = np.asarray(w)
        return w.reshape(w.shape[0], NP, 2, DH).transpose(0, 2, 3, 1).reshape(w.shape[0], H * DH)

    def halves(w):
        w = np.asarray(w)
        return w.reshape(w.shape[0], NP, 2, DH).transpose(0, 2, 1, 3).reshape(w.shape[0], H * DH)

    w1, w2, b1 = (np.asarray(a) for a in (L0_ffn_W1, L0_ffn_W2, L0_ffn_b1))
    w_experts = np.concatenate([w1, w2.reshape(E, NC_H, P, D).transpose(0, 2, 1, 3).reshape(E, P, NC_H * D),
                                b1.reshape(E, NC_H, P).transpose(0, 2, 1)], axis=2)
    const_f32, const_bf16, q_rows, k_rows = shape_constants()
    arrays = {
        "x": L0_attn_x,
        "wq_t": pair_order(np.asarray(L0_attn_Wq).T), "wk_t": pair_order(np.asarray(L0_attn_Wk).T), "wv_t": halves(np.asarray(L0_attn_Wv).T),
        "aq_t": pair_order(np.asarray(L0_attn_Aq).T), "ak_t": pair_order(np.asarray(L0_attn_Ak).T), "av_t": halves(np.asarray(L0_attn_Av).T),
        "bq": L0_attn_Bq, "bk": L0_attn_Bk, "bv": L0_attn_Bv, "wp_t": np.asarray(L0_attn_Wp).T,
        "wr": L0_ffn_Wr, "br": L0_ffn_br, "w_experts": w_experts, "b2": L0_ffn_b2,
        "const_f32": const_f32, "const_bf16": const_bf16, "q_const_rows": q_rows, "k_const_rows": k_rows,
    }
    arrays = {n: np.ascontiguousarray(a) for n, a in arrays.items()}
    nc = bacc.Bacc("TRN2", target_bir_lowering=False, num_devices=1)
    args = [nc.dram_tensor(n, a.shape, mybir.dt.from_np(a.dtype), kind="ExternalInput").ap() for n, a in arrays.items()]
    out = nc.dram_tensor("out", (NB, T, D), F32, kind="ExternalOutput").ap()
    program(nc, *args, out)
    r = run_bass_kernel_spmd(nc, [arrays], core_ids=[0])
    return r.results[0]["out"]
```

```python
from contextlib import ExitStack

import numpy as np
import concourse.bass as bass
import concourse.mybir as mybir

F32 = mybir.dt.float32
BF16 = mybir.dt.bfloat16
I32 = mybir.dt.int32
U32 = mybir.dt.uint32
ALU = mybir.AluOpType
ACT = mybir.ActivationFunctionType
AX = mybir.AxisListType

P = 128
NB, T, D = 16, 256, 128
NT = NB * T // P
H, DH = 16, 8
NP = H // 2
BLK = 64
NBLK = T // BLK
RANK = 8
LORA_SCALE = 16 / RANK
E, HID = 8, 512
VL = BLK + E
NC_H = HID // P
WE = HID + NC_H * D + NC_H
SUM_STEPS = (E * NC_H).bit_length() - 1
WB = WE + 2 * NC_H
SLOT_TILES = (NB * T + E * (P - 1)) // P
EPS = 1e-5
LN_GROUPS = (slice(0, NT // 4), slice(NT // 4, NT // 2), slice(NT // 2, NT))
NEG = -1e30

PLACES_Q = (slice(0, 3), slice(3, 6, 2), slice(4, 5))
PLACES_K = (slice(2, 5), slice(0, 6, 5), slice(1, 2))
TERMS = 6
CONST_ROW = 48
MAX_ROW = 54
LOADS = 4

UNITS = ([(3, (p, p + 1)) for p in range(0, NP, 2)] + [(2, (p, p + 1)) for p in range(0, NP, 2)]
         + [(1, tuple(range(p, p + 4))) for p in (0, 4)] + [(0, tuple(range(NP)))])
NU = len(UNITS)
PV_AFTER = {1: (0, 1), 3: (2, 3), 5: (4, 5), 7: (6, 7), 8: (8,), 9: (9,), 10: (10,)}
NPV = len(PV_AFTER)
PV_OF = {w: n for n, units in enumerate(PV_AFTER.values()) for w in units}
BESIDE = NB - 8
EARLY_UNITS = {b: [(m // NU, m % NU) for m in range(2 * NU * n // (NB - BESIDE), 2 * NU * (n + 1) // (NB - BESIDE))]
               for n, b in enumerate(range(BESIDE, NB))}
CHOSEN = NB - 4

TURNS = SLOT_TILES // 3
EXPERTS_AFTER, GATE_STEP, GATE_TILES = 4, 5, 3
GATE_CHUNKS = {GATE_STEP + c: (GATE_TILES * c, GATE_TILES * (c + 1)) for c in range(8)} | {13: (24, 26), 14: (26, 32)}
GATHERED = {i: min(4 * (i - EXPERTS_AFTER) + 2 * GATE_TILES, NT) for i in range(EXPERTS_AFTER, NB)}
GATE_AT = 6
GATE_PIECES = (8, 10)
GATE_STEPS = list(GATE_CHUNKS)
GATE_OF = {n: c for c, (n0, n1) in enumerate(GATE_CHUNKS.values()) for n in range(n0, n1)}
RESIDUAL_STEP = [max(b + 2, GATE_STEPS[GATE_OF[2 * b + 1]]) for b in range(NB)]


def program(nc, x, w_dense, lora, br, w_experts, const_f32, const_bf16, q_const_rows, k_const_rows, out):
    x_tiles = x.rearrange("b (j p) d -> p (b j) d", p=P)
    out_tiles = out.rearrange("b (j p) d -> p (b j) d", p=P)
    qk_dram = nc.dram_tensor("qk_parts", [NB, 2, TERMS, P, T], BF16).ap()
    xs_dram = nc.dram_tensor("sorted_rows", [SLOT_TILES * P, D], F32).ap()
    y_dram = nc.dram_tensor("expert_rows", [SLOT_TILES * P, D], F32).ap()

    const_bf16, q_const_rows, k_const_rows = (a.bitcast(BF16) for a in (const_bf16, q_const_rows, k_const_rows))

    ctx = ExitStack()
    with ctx:
        def sb(name, shape, dt=F32):
            return ctx.enter_context(nc.sbuf_tensor(name, shape, dt))

        def sem(name):
            return ctx.enter_context(nc.semaphore(name))

        bank = [ctx.enter_context(nc.psum_tensor(f"bank{i}", [P, 512], F32)) for i in range(8)]

        cf = sb("cf", [P, 2 * P + 64])
        ident_f = cf[:, 0:P]
        ones_f = cf[:, P:2 * P]
        iota8 = cf[:, 2 * P:2 * P + 8]
        iota_tile = cf[0:1, 2 * P + 8:2 * P + 8 + SLOT_TILES]
        of_half = cf[:, 2 * P + 50:2 * P + 52]
        cb = sb("cb", [P, 2 * BLK + 2 * P + 2 * (NT + 1) * E + 2], BF16)
        mask_qk = cb[:, 0:BLK]
        mask_kq = cb[:, BLK:2 * BLK]
        ident_b = cb[:, 2 * BLK:2 * BLK + P]
        before_b = cb[:, 2 * BLK + P:2 * BLK + 2 * P]
        later_b = cb[:, 2 * BLK + 2 * P:2 * BLK + 2 * P + 2 * (NT + 1) * E].rearrange("p (h c) -> p h c", h=2)
        one_b = cb[:, 2 * BLK + 2 * P + 2 * (NT + 1) * E:2 * BLK + 2 * P + 2 * (NT + 1) * E + 1]
        dense = sb("dense", [P, 4 * P + E])
        w_raw = dense[:, 0:3 * P].rearrange("p (n d) -> p n d", n=3)
        wp_sb = dense[:, 3 * P:4 * P]
        wr_sb = dense[:, 4 * P:4 * P + E]
        w_eff = sb("w_eff", [P, 2, P])
        w_v = sb("w_v", [P, 2, BLK + E])
        w_v_flat = w_v[:, :, :].rearrange("p a x -> p (a x)")
        lora_sb = sb("lora_sb", [RANK, 7 * P])
        lora_a, lora_b = (lora_sb[:, 3 * n * P:3 * (n + 1) * P].rearrange("p (n d) -> p n d", n=3) for n in range(2))
        b2_sb = lora_sb[:, 6 * P:7 * P]
        br_sb = sb("br_sb", [P, E])
        zeros = sb("zeros", [P, D])

        x_all = sb("x_all", [P, NT, D])
        xn_all = sb("xn_all", [P, NT, D])
        v_all = sb("v_all", [P, NB, NBLK, NP, DH])
        s_all = v_all[:, :, :, :, :].rearrange("p b n h d -> p (b n h d)").rearrange("p (t d) -> p t d", d=D)
        stats = sb("stats", [P, NT, 6])
        ln = sb("ln", [P, 8, NT])
        rstd, nmr = sb("rstd", [P, NT]), sb("nmr", [P, NT])
        xn_slot = sb("xn_slot", [P, 2, 2, D])
        xnT_slot = sb("xnT_slot", [P, 2, T])
        w_slots = sb("w_slots", [P, 3, WB])
        w_slot = [w_slots[:, r] for r in range(3)]
        slots_flat = w_slots[:, :, :].rearrange("p r f -> p (r f)")
        rem = slots_flat[:, 0:4 * T].rearrange("p (r x) -> p r x", r=2)
        parts = slots_flat[:, 4 * T:10 * T].bitcast(BF16).rearrange("p (r c s t) -> p r c s t", r=2, c=3, s=2)

        logits = sb("logits", [P, NT, E])
        onehot_b = sb("onehot_b", [P, NT, E], BF16)
        tile_counts = sb("tile_counts", [P, 2, P], BF16)
        r32 = sb("r32", [P, 4, NT])
        r8 = sb("r8", [P, 8, E])
        r8i = sb("r8i", [P, 2, E], I32)
        slot_of = sb("slot_of", [P, NT], U32)
        te_cmp = sb("te_cmp", [1, SLOT_TILES, E])
        te_f = sb("te_f", [1, 2, SLOT_TILES])
        tile_expert = sb("tile_expert", [1, SLOT_TILES], I32)

        q_plain_all, k_plain_all = sb("q_plain", [P, 2, NP, T], BF16), sb("k_plain", [P, 2, NP, T], BF16)
        q_plain, k_plain = ([a[:, r] for r in range(2)] for a in (q_plain_all, k_plain_all))
        q_diag_all, k_diag_all = sb("q_diag", [P, 2, NP, 2, T], BF16), sb("k_diag", [P, 2, NP, 2, T], BF16)
        q_diag, k_diag = ([a[:, r] for r in range(2)] for a in (q_diag_all, k_diag_all))
        v_diag = [sb(f"v_diag{r}", [P, NBLK, NP, 32]) for r in range(2)]
        v_halves = [v[:, :, :, :].rearrange("p n h (c d) -> p (n h) c d", c=2) for v in v_diag]
        probs = sb("probs", [P, NU, 512])
        row_max = [sb(f"row_max{r}", [P, NBLK, NP]) for r in range(2)]
        nmax = [sb(f"nmax{r}", [P, NBLK, 3, NP], BF16) for r in range(2)]
        nmax_rem = sb("nmax_rem", [P, NBLK, NP])
        nmaxT = [sb(f"nmaxT{r}", [3 * NP, 2 * T], BF16) for r in range(2)]
        oT = sb("oT", [P, 512])
        rz = sb("rz", [P, 2 * H])
        o_tok = sb("o_tok", [P, 2, D])
        o2T = sb("o2T", [P, 2 * P])

        w_all = sb("w_all", [P, E, WB])
        xs_slot = xn_slot[:, :, :, :].rearrange("p r j d -> p (r j) d")[:, 0:3]
        xsT_slot = xnT_slot[:, :, :].rearrange("p r (j k) -> p (r j) k", k=P)[:, 0:3]
        hT = sb("hT", [P, 3, NC_H, P])
        rt = hT[:, :, :, :].rearrange("p r c k -> p (r c k)").rearrange("p (c n) -> p c n", c=6)
        y_slot = sb("y_slot", [P, 3, D])
        c_bc = sb("c_bc", [P, D])
        rb1 = sb("rb1", [P, E, NC_H])
        y_tok = xn_all
        gate_e = [w_slot[r][:, 0:8 * D] for r in range(2)]

        names = """weights_in x_in0 x_in1 x_in2 x_in3 zero_src zeros_out lora_ps w_eff_done experts_in
            crelu c_sum c_bc_ps c_bc_done var_done std_done dve_seq
            xn_done xn_kept xT_ps xT_done qk_ps lg_ps part1_done rem_done part2_done part3_done v_done lg_done
            qk1_out0 qk1_out1 qk2_out0 qk2_out1 qk3_out0 qk3_out1
            const_rows_in diag_zero vd_zero vd_one onehot_done rank_ps counts_done slots_done tile_expert_done scattered
            qd_ks_in0 qd_ks_in1 qs_kd_in0 qs_kd_in1 max_in0 max_in1 s_ps max_done mT_ps nmax1 nmax_r nmax2 nmax3 nmaxT_done
            vdiag_done st_ps exp_done pv_ps oT_done otok_ps rz_done otok_done o2T_ps o2T_done s_out_ps s_done
            w_done xs_in0 xs_in1 xs_in2 xsT_ps xsT_done h_ps bias_done h_done y_ps y_done
            gathered gate_in_done gate_exp_done gate_sum_done gate_recip_done gate_done gated_done res_done last_done y_out0 y_out1 y_out2 stored""".split()
        S = {n: sem(n) for n in names}

        def wait(eng, name, value):
            if not isinstance(value, int) or value > 0:
                eng.wait_ge(S[name], value)

        def lens(unit):
            n, pairs = UNITS[unit]
            return n, pairs, BLK * (n + 1)

        def attention_steps(body, eng, experts=None):
            body(0, 0, False)
            with eng.Fori(0, EXPERTS_AFTER // 2) as k:
                body(k * 2 + 1, 1, False)
                body(k * 2 + 2, 0, False)
            if experts:
                experts()
            with eng.Fori(EXPERTS_AFTER // 2, 6) as k:
                body(k * 2 + 1, 1, True)
                body(k * 2 + 2, 0, True)
            for i in (13, 14, 15):
                body(i, i % 2, i in GATE_CHUNKS)

        def in_four_banks(b):
            return isinstance(b, int) and b >= NB - 2

        def max_at(i):
            return 1 if in_four_banks(i) else 4

        def score_bank(b, r, u):
            return bank[(0, 2, 1, 3)[((b - NB + 2) * NU + u) % 4]] if in_four_banks(b) else bank[2 + (u + r) % 2]

        def has(i, low, high):
            return not isinstance(i, int) or low <= i <= high

        def projection_steps(turn, project, eng, statistics=None, beside=None):
            turn(0, 0, True)
            turn(1, 1, True)
            for b in range(4):
                project(b, b % 2, b < 2)
                if b < 3:
                    turn(b + 2, b % 2, False)
                if statistics and b in (0, 3):
                    statistics(1 + b // 3)
            with eng.Fori(2, BESIDE // 2) as k:
                turn(k * 2 + 1, 1, False)
                project(k * 2, 0, False)
                turn(k * 2 + 2, 0, False)
                project(k * 2 + 1, 1, False)
            for b in range(BESIDE, NB):
                if b + 1 < NB:
                    turn(b + 1, (b + 1) % 2, False)
                project(b, b % 2, False)
                if beside:
                    for n, u in EARLY_UNITS[b]:
                        beside(n, u)

        block = ctx.enter_context(nc.Block())

        @block.sync
        def _(sp):
            for c in range(4):
                tiles = slice(c * NT // 4, (c + 1) * NT // 4)
                sp.dma_start(x_all[:, tiles, :], x_tiles[:, tiles, :]).then_inc(S[f"x_in{c}"], 16)
                if c == 1:
                    for dst, src in ((dense[:, :], w_dense), (lora_sb[:, :], lora), (cf[:, :], const_f32),
                                     (br_sb[:, :], br.partition_broadcast(P)), (cb[:, :], const_bf16)):
                        sp.dma_start(dst, src).then_inc(S["weights_in"], 16)
            stacks = ((q_plain_all, q_diag_all, q_const_rows), (k_plain_all, k_diag_all, k_const_rows))
            const_rows = [slice(64 * a + CONST_ROW, 64 * a + 64) for a in range(2)]
            for plain, diag, src in stacks:
                for a, rows in enumerate(const_rows):
                    sp.dma_start(plain[rows].rearrange("x r p t -> x (r p t)"), src[a]).then_inc(S["const_rows_in"], 16)

            sp.wait_ge(S["zero_src"], 1)
            sp.dma_start(xs_dram.rearrange("(p r) d -> p r d", p=P),
                         zeros[:, :].unsqueeze(1).to_broadcast([P, SLOT_TILES, D])).then_inc(S["zeros_out"], 16)

            def diag_const_rows():
                sp.wait_ge(S["diag_zero"], 2)
                for plain, diag, src in stacks:
                    for a, rows in enumerate(const_rows):
                        sp.dma_start(diag[rows, :, :, a].rearrange("x r p t -> x (r p) t"),
                                     src[a].rearrange("x (n t) -> x n t", t=T)).then_inc(S["const_rows_in"], 16)

            def store_parts(b, r):
                for part in range(2):
                    sp.wait_ge(S[f"part{part + 1}_done"], b + 1)
                    for s, places in enumerate((PLACES_Q, PLACES_K)):
                        dst = qk_dram[bass.ds(b, 1), s, places[part]].rearrange("o c p t -> p (o c) t")
                        copies = len(range(*places[part].indices(TERMS)))
                        sp.dma_start(dst, parts[:, r, part, s].unsqueeze(1).to_broadcast([P, copies, T])).then_inc(S[f"qk{part + 1}_out{r}"], 16)

            def load_stack(dst, diag, is_q, b, name):
                for a in range(2):
                    src = qk_dram[bass.ds(b, 1), 0 if is_q else 1, :, 64 * a:64 * a + 64].rearrange("o c x t -> (o c) x t")
                    rows = slice(64 * a, 64 * a + CONST_ROW)
                    if diag:
                        sp.dma_start(dst[rows, :, a], src).then_inc(S[name], 16)
                    else:
                        sp.dma_start(dst[rows].rearrange("r p t -> r (p t)"),
                                     src.rearrange("c (d p) t -> c d (p t)", p=NP)).then_inc(S[name], 16)

            def load_for_max(b, r):
                load_stack(q_diag[r], True, True, b, f"qd_ks_in{r}")
                load_stack(k_plain[r], False, False, b, f"qd_ks_in{r}")

            def load_for_probs(b, r):
                load_stack(q_plain[r], False, True, b, f"qs_kd_in{r}")
                load_stack(k_diag[r], True, False, b, f"qs_kd_in{r}")

            def load_max_rows(b, r):
                sp.wait_ge(S["nmaxT_done"], b + 1)
                for a in range(2):
                    rows = slice(64 * a + MAX_ROW, 64 * a + MAX_ROW + 3)
                    sp.dma_start(q_plain[r][rows], nmaxT[r][:, a * T:(a + 1) * T]).then_inc(S[f"max_in{r}"], 16)

            def store_batches(k0, k1):
                if k1 - k0 == 1:
                    for r in range(2):
                        store_parts(k0 * 2 + r, r)
                else:
                    with sp.Fori(k0, k1) as k:
                        for r in range(2):
                            store_parts(k * 2 + r, r)

            store_batches(0, 1)
            diag_const_rows()
            store_batches(1, 2)
            sp.wait_ge(S["const_rows_in"], 16 * 8)
            for r in range(2):
                sp.wait_ge(S[f"qk3_out{r}"], 16)
                sp.wait_ge(S[f"qk1_out{r}"], 32)
                sp.wait_ge(S[f"qk2_out{r}"], 32)
            load_for_max(0, 0)
            store_batches(2, 4)
            load_for_max(1, 1)
            store_batches(4, 6)
            load_for_probs(0, 0)
            store_batches(6, 7)
            load_max_rows(0, 0)
            sp.wait_ge(S["qk3_out0"], 32)
            sp.wait_ge(S["qk1_out0"], 64)
            sp.wait_ge(S["qk2_out0"], 64)
            load_for_max(2, 0)
            store_parts(NB - 2, 0)
            store_parts(NB - 1, 1)
            for r in range(2):
                sp.wait_ge(S[f"qk3_out{r}"], 16 * NB // 2)
                sp.wait_ge(S[f"qk1_out{r}"], 32 * NB // 2)
                sp.wait_ge(S[f"qk2_out{r}"], 32 * NB // 2)

            def load_expert(e):
                sp.dma_start(w_all[:, bass.ds(e, 1), 0:WE].rearrange("p o f -> p (o f)"),
                             w_experts[bass.ds(e, 1)].rearrange("o p f -> (o p) f")).then_inc(S["experts_in"], 16)

            def store_out(b0, b1):
                if b1 < NB:
                    sp.wait_ge(S["res_done"], b1)
                else:
                    sp.wait_ge(S["last_done"], 1)
                tiles = slice(2 * b0, 2 * b1)
                sp.dma_start(out_tiles[:, tiles, :], s_all[:, tiles, :]).then_inc(S["stored"], 16)

            def step(i, r, gate):
                if not isinstance(i, int) and not gate:
                    for n in range(2):
                        load_expert(i * 2 + n - 2)
                if has(i, 0, 14):
                    wait(sp, "st_ps", i * NU)
                    load_for_probs(i + 1, 1 - r)
                if has(i, 0, 12):
                    sp.wait_ge(S["s_ps"], (i + 2) * NU)
                    load_for_max(i + 3, 1 - r)
                if has(i, 0, 14):
                    load_max_rows(i + 1, 1 - r)
                if isinstance(i, int) and i >= 13:
                    store_out(*{13: (0, 10), 14: (10, 12), 15: (12, 13)}[i])

            def experts():
                sp.wait_ge(S["scattered"], 16 * NT)

                def load_rows(t, r):
                    wait(sp, "xsT_ps", t - 2)
                    sp.dma_start(xs_slot[:, r, :], xs_dram[bass.ds(t * P, P), :]).then_inc(S[f"xs_in{r}"], 16)

                def store_y(t, r):
                    sp.wait_ge(S["y_done"], t + 1)
                    sp.dma_start(y_dram[bass.ds(t * P, P), :], y_slot[:, r, :]).then_inc(S[f"y_out{r}"], 16)
                for t in range(5):
                    load_rows(t, t % 3)
                load_rows(5, 2)
                store_y(0, 0)
                with sp.Fori(1, TURNS - 1) as k:
                    for r in range(3):
                        load_rows(k * 3 + r + 3, r)
                        store_y(k * 3 + r - 2, (r + 1) % 3)
                for t in range(SLOT_TILES - 5, SLOT_TILES):
                    store_y(t, t % 3)
            attention_steps(step, sp, experts)
            for b in (13, 14, 15):
                store_out(b, b + 1)
            sp.wait_ge(S["stored"], 6 * 16)

        @block.gpsimd
        def _(pool):
            pool.memset(zeros[:, :], 0.0).then_inc(S["zero_src"], 1)
            for diag in (q_diag_all, k_diag_all):
                pool.memset(diag[:, :, :, :, :], 0.0).then_inc(S["diag_zero"], 1)
            for r in range(2):
                pool.memset(v_diag[r][:, :, :, :], 0.0).then_inc(S["vd_zero"], 1)
            pool.wait_ge(S["vd_zero"], 2)
            pool.wait_ge(S["weights_in"], 16 * 5)
            for r in range(2):
                pool.tensor_copy(v_halves[r][:, :, :, DH], of_half.unsqueeze(1).to_broadcast([P, NBLK * NP, 2])).then_inc(S["vd_one"], 1)
            pool.wait_ge(S["vd_one"], 2)

            def third_part(b, r, first):
                if not first:
                    pool.wait_ge(S[f"qk3_out{r}"], (b - r) * 8)
                pool.wait_ge(S["part2_done"], b + 1)
                pool.tensor_tensor(parts[:, r, 2], rem[:, r].rearrange("p (s t) -> p s t", s=2), parts[:, r, 1], ALU.subtract).then_inc(S["part3_done"], 1)
                pool.wait_ge(S["part3_done"], b + 1)
                pool.wait_ge(S["vd_one"], 2)
                both = qk_dram[bass.ds(b, 1)].rearrange("o s c p t -> p (o s c) t")
                first, second = PLACES_Q[2].start, TERMS + PLACES_K[2].start
                pool.dma_start(both[:, first:second + 1:second - first], parts[:, r, 2]).then_inc(S[f"qk3_out{r}"], 16)
            def spread_v(b, r):
                v = v_all[:, bass.ds(b, 1)].rearrange("p o n h d -> p (o n h) d")
                pool.tensor_tensor(v_halves[r][:, :, :, 0:DH], v.unsqueeze(2).to_broadcast([P, NBLK * NP, 2, DH]),
                                   of_half.unsqueeze(1).unsqueeze(3).to_broadcast([P, NBLK * NP, 2, DH]),
                                   ALU.mult).then_inc(S["vdiag_done"], 1)

            def beside(n, u):
                if u == NU // 2:
                    spread_v(n, n)
            projection_steps(lambda b, r, first: None, third_part, pool, None, beside)

            def scatter(tiles):
                for n in tiles:
                    pool.indirect_dma_start(xs_dram[:, :], bass.IndirectOffsetOnAxis(slot_of[:, n:n + 1], axis=0),
                                            xn_all[:, n, :], None).then_inc(S["scattered"], 16)

            def gather(tiles):
                for n in tiles:
                    pool.indirect_dma_start(y_tok[:, n, :], None, y_dram[:, :],
                                            bass.IndirectOffsetOnAxis(slot_of[:, n:n + 1], axis=0)).then_inc(S["gathered"], 16)

            def pre_gate(c):
                n0, n1 = GATE_CHUNKS[GATE_STEPS[c]]
                pool.tensor_tensor(y_tok[:, n0:n1, :], y_tok[:, n0:n1, :],
                                   c_bc[:, :].unsqueeze(1).to_broadcast([P, n1 - n0, D]), ALU.add).then_inc(S["gate_in_done"], 1)

            def gate_product(c):
                n0, n1 = GATE_CHUNKS[GATE_STEPS[c]]
                pool.wait_ge(S["gate_recip_done"], len(GATE_PIECES) * (c + 1))
                pool.tensor_tensor(y_tok[:, n0:n1, :], y_tok[:, n0:n1, :],
                                   gate_e[GATE_STEPS[c] % 2][:, 0:(n1 - n0) * D].rearrange("p (j d) -> p j d", d=D), ALU.mult).then_inc(S["gate_done"], 1)

            def residual(b):
                tiles = slice(2 * b, 2 * b + 2)
                pool.wait_ge(S["s_done"], b + 1)
                pool.wait_ge(S["gate_done"], GATE_OF[2 * b + 1] + 1)
                pool.tensor_tensor(s_all[:, tiles, :], s_all[:, tiles, :], y_tok[:, tiles, :], ALU.mult).then_inc(S["gated_done"], 1)
                pool.wait_ge(S["gated_done"], b + 1)
                pool.tensor_tensor(s_all[:, tiles, :], s_all[:, tiles, :], x_all[:, tiles, :], ALU.add).then_inc(S["res_done"], 1)

            def sum_unselected():
                pool.wait_ge(S["crelu"], 1)
                pool.wait_ge(S["scattered"], 16 * NT)
                terms = xn_all[:, 0:E * NC_H, :]
                pool.tensor_tensor(terms.rearrange("p (e c) d -> p e c d", e=E),
                                   w_all[:, :, HID:HID + NC_H * D].rearrange("p e (c d) -> p e c d", c=NC_H),
                                   rb1[:, :, :].unsqueeze(3).to_broadcast([P, E, NC_H, D]), ALU.mult).then_inc(S["c_sum"], 1)
                for n in range(SUM_STEPS):
                    half = E * NC_H >> (n + 1)
                    pool.wait_ge(S["c_sum"], n + 1)
                    pool.tensor_tensor(terms[:, 0:half, :], terms[:, 0:half, :], terms[:, half:2 * half, :], ALU.add).then_inc(S["c_sum"], 1)

            for i in range(NB):
                for b in {0: (), EXPERTS_AFTER: (i + 1, i + 2), EXPERTS_AFTER + 1: ()}.get(i, (i + 1,)):
                    if b < NB:
                        wait(pool, "pv_ps", (b - 1) * NPV)
                        spread_v(b, b % 2)
                if i == 0:
                    pool.wait_ge(S["slots_done"], 1)
                    pool.wait_ge(S["zeros_out"], 16)
                    pool.wait_ge(S["xn_kept"], NB)
                if i < EXPERTS_AFTER:
                    scatter(range(i * NT // EXPERTS_AFTER, (i + 1) * NT // EXPERTS_AFTER))
                if i == EXPERTS_AFTER:
                    sum_unselected()
                    pool.wait_ge(S["c_bc_done"], 1)
                    for r in range(3):
                        pool.wait_ge(S[f"y_out{r}"], 16 * TURNS)
                    gather(range(GATE_TILES))
                if i + 1 in GATE_CHUNKS:
                    pool.wait_ge(S["gathered"], 16 * GATHERED.get(i - 1, GATE_TILES))
                    pre_gate(GATE_STEPS.index(i + 1))
                if i >= EXPERTS_AFTER:
                    gather(range(GATHERED.get(i - 1, GATE_TILES), GATHERED[i]))
                if i in GATE_CHUNKS:
                    gate_product(GATE_STEPS.index(i))
                for b in range(NB):
                    if RESIDUAL_STEP[b] == i:
                        residual(b)
            residual(NB - 2)

        @block.scalar
        def _(act):
            def deviation(group):
                g = LN_GROUPS[group]
                act.wait_ge(S["var_done"], group + 1)
                act.activation(ln[:, 4, g], ln[:, 3, g], ACT.Sqrt).then_inc(S["std_done"], 1)
            deviation(0)

            def turn_x(b, r, first):
                act.wait_ge(S["xT_ps"], b + 1)
                if not first:
                    act.wait_ge(S["lg_ps"], b - 1)
                act.activation(xnT_slot[:, r, :], bank[r][:, 0:T], ACT.Copy).then_inc(S["xT_done"], 1)
                act.wait_ge(S["xn_done"], 2 * b + 2)
                act.activation(xn_all[:, bass.ds(b * 2, 2), :], xn_slot[:, r], ACT.Copy).then_inc(S["xn_kept"], 1)

            def evacuate(b, r, first):
                act.wait_ge(S["qk_ps"], b + 1)
                if not first:
                    act.wait_ge(S[f"qk1_out{r}"], (b - r) * 16)
                act.activation(parts[:, r, 0], bank[2 + r][:, :].rearrange("p (s t) -> p s t", s=2), ACT.Copy).then_inc(S["part1_done"], 1)
                act.wait_ge(S["lg_ps"], b + 1)
                act.activation(v_all[:, bass.ds(b, 1)].rearrange("p o n h d -> p (o n) (h d)"),
                               bank[4 + r][:, 0:NBLK * VL].rearrange("p (n x) -> p n x", x=VL)[:, :, 0:BLK], ACT.Copy).then_inc(S["v_done"], 1)
                act.wait_ge(S["rem_done"], b + 1)
                if not first:
                    act.wait_ge(S[f"qk2_out{r}"], (b - r) * 16)
                act.activation(parts[:, r, 1], rem[:, r].rearrange("p (s t) -> p s t", s=2), ACT.Copy).then_inc(S["part2_done"], 1)
            def max_rows(b, r):
                act.wait_ge(S["mT_ps"], b + 1)
                if has(b, 2, 15):
                    act.wait_ge(S[f"max_in{r}"], (b - r) * 16)
                act.activation(nmaxT[r][:, :], bank[5][0:3 * NP, :], ACT.Copy).then_inc(S["nmaxT_done"], 1)

            def early(n, u):
                if (n, u) == (1, 1):
                    max_rows(0, 0)
            projection_steps(turn_x, evacuate, act, deviation, early)

            def out_o2T(b):
                act.wait_ge(S["o2T_ps"], b + 1)
                act.activation(o2T[:, :], bank[7][:, 0:2 * P], ACT.Copy).then_inc(S["o2T_done"], 1)

            def out_s(b):
                act.wait_ge(S["s_out_ps"], b + 1)
                act.activation(s_all[:, bass.ds(b * 2, 2), :], bank[7][:, 2 * P:4 * P].rearrange("p (j d) -> p j d", d=D),
                               ACT.Copy).then_inc(S["s_done"], 1)

            def gate_exp(i, r):
                if isinstance(i, int):
                    (n0, n1), c = GATE_CHUNKS[i], GATE_STEPS.index(i)
                    tiles, width = slice(n0, n1), n1 - n0
                else:
                    c = i - GATE_STEP
                    tiles, width = bass.ds(c * GATE_TILES, GATE_TILES), GATE_TILES
                act.wait_ge(S["gate_in_done"], c + 1)
                act.wait_ge(S["y_done"], SLOT_TILES)
                act.activation(gate_e[r][:, 0:width * D].rearrange("p (j d) -> p j d", d=D), y_tok[:, tiles, :],
                               ACT.Exp, scale=-1.0).then_inc(S["gate_exp_done"], 1)

            def gate_sum(i, r):
                c, n = (GATE_STEPS.index(i), GATE_CHUNKS[i][1] - GATE_CHUNKS[i][0]) if isinstance(i, int) else (i - GATE_STEP, GATE_TILES)
                act.wait_ge(S["gate_exp_done"], c + 1)
                act.activation(gate_e[r][:, 0:n * D], gate_e[r][:, 0:n * D], ACT.Copy, bias=1.0).then_inc(S["gate_sum_done"], 1)

            def step(i, r, gate):
                for u in range(NU):
                    n, pairs, ln_u = lens(u)
                    w = ln_u * len(pairs)
                    act.wait_ge(S["st_ps"], i * NU + u + 1)
                    wait(act, "pv_ps", (i - 1) * NPV + PV_OF[u] + 1)
                    act.activation(probs[:, u, 0:w], score_bank(i, r, u)[:, 0:w], ACT.Exp).then_inc(S["exp_done"], 1)
                    if has(i, 0, 14) and u == max_at(i) + 1:
                        max_rows(i + 1, 1 - r)
                    if isinstance(i, int) and i == 0 and u == 1:
                        act.wait_ge(S["rank_ps"], 1)
                        act.activation(tile_counts[:, :, :], bank[7][:, 384:386].unsqueeze(2).to_broadcast([P, 2, P]), ACT.Copy).then_inc(S["counts_done"], 1)
                    if has(i, 1, 15):
                        if u == 8:
                            out_o2T(i - 1)
                        if u == NU - 1:
                            out_s(i - 1)
                    if gate and u == GATE_AT:
                        gate_exp(i, r)
                    if gate and u == GATE_AT + 1:
                        gate_sum(i, r)
                act.wait_ge(S["pv_ps"], (i + 1) * NPV)
                wait(act, "otok_ps", i)
                act.activation(oT[:, :], bank[4][:, :], ACT.Copy).then_inc(S["oT_done"], 1)

            def experts():
                def turn_rows(t, r):
                    act.wait_ge(S["xsT_ps"], t + 1)
                    wait(act, "h_ps", t - 2)
                    act.activation(xsT_slot[:, r, :], bank[6][:, r * P:(r + 1) * P], ACT.Copy).then_inc(S["xsT_done"], 1)

                def copy_weights(t, r):
                    e = act.value_load(tile_expert[0:1, bass.ds(t, 1)], min_val=0, max_val=E - 1)
                    wait(act, "y_ps", t - 2)
                    act.activation(w_slot[r], w_all[:, bass.ds(e, 1), :].rearrange("p o f -> p (o f)"), ACT.Copy).then_inc(S["w_done"], 1)

                turn_rows(0, 0)
                act.wait_ge(S["tile_expert_done"], 1)
                act.wait_ge(S["bias_done"], 2)
                copy_weights(0, 0)
                turn_rows(1, 1)
                copy_weights(1, 1)
                act.activation(rb1[:, :, :], w_all[:, :, HID + NC_H * D:WE], ACT.Relu).then_inc(S["crelu"], 1)
                turn_rows(2, 2)
                copy_weights(2, 2)
                with act.Fori(1, TURNS) as k:
                    for r in range(3):
                        turn_rows(k * 3 + r, r)
                        copy_weights(k * 3 + r, r)
                act.wait_ge(S["c_bc_ps"], 1)
                act.activation(c_bc[:, :], bank[7][:, 0:D], ACT.Copy).then_inc(S["c_bc_done"], 1)
            attention_steps(step, act, experts)
            out_o2T(NB - 1)

        @block.vector
        def _(dve):
            seq = [0]

            def then(ins):
                seq[0] += 1
                ins.then_inc(S["dve_seq"], 1)
                dve.wait_ge(S["dve_seq"], seq[0])

            def moments(c):
                dve.wait_ge(S[f"x_in{c}"], 16)
                for n in range(c * NT // 4, (c + 1) * NT // 4):
                    last = dve.bn_stats(stats[:, n, :], x_all[:, n, :])
                then(last)

            def statistics(group):
                g = LN_GROUPS[group]
                mean_e, m2_e, mean_o, m2_o = (stats[:, g, c] for c in (1, 2, 4, 5))
                dve.tensor_tensor(ln[:, 0, g], mean_e, mean_o, ALU.add)
                dve.tensor_tensor(ln[:, 1, g], mean_e, mean_o, ALU.subtract)
                then(dve.tensor_tensor(ln[:, 2, g], m2_e, m2_o, ALU.add))
                then(dve.tensor_tensor(ln[:, 1, g], ln[:, 1, g], ln[:, 1, g], ALU.mult))
                then(dve.tensor_scalar(ln[:, 2, g], ln[:, 2, g], 1.0 / D, EPS, ALU.mult, ALU.add))
                dve.scalar_tensor_tensor(ln[:, 3, g], ln[:, 1, g], 0.25, ln[:, 2, g], ALU.mult, ALU.add).then_inc(S["var_done"], 1)
                dve.wait_ge(S["std_done"], group + 1)
                then(dve.reciprocal(ln[:, 5, g], ln[:, 4, g]))
                then(dve.tensor_tensor(ln[:, 6, g], ln[:, 5, g], ln[:, 5, g], ALU.mult))
                then(dve.tensor_tensor(ln[:, 6, g], ln[:, 6, g], ln[:, 3, g], ALU.mult))
                then(dve.tensor_scalar(ln[:, 6, g], ln[:, 6, g], -0.5, 1.5, ALU.mult, ALU.add))
                then(dve.tensor_tensor(rstd[:, g], ln[:, 5, g], ln[:, 6, g], ALU.mult))
                then(dve.scalar_tensor_tensor(nmr[:, g], ln[:, 0, g], -0.5, rstd[:, g], ALU.mult, ALU.mult))
            moments(0)
            statistics(0)

            dve.wait_ge(S["lora_ps"], 1)
            for n in range(3):
                dst = w_eff[:, n, :] if n < 2 else w_v[:, :, 0:BLK]
                parts_of = (lambda a: a) if n < 2 else (lambda a: a.rearrange("p (a x) -> p a x", a=2))
                last = dve.scalar_tensor_tensor(dst, parts_of(bank[0][:, n * P:(n + 1) * P]), LORA_SCALE, parts_of(w_raw[:, n, :]),
                                                ALU.mult, ALU.add)
            dve.tensor_copy(w_v[:, 0, BLK:], wr_sb)
            then(last)
            dve.tensor_scalar(w_eff[:, 0, :], w_eff[:, 0, :], float(DH) ** -0.5, None, ALU.mult).then_inc(S["w_eff_done"], 1)

            def normalise(b, r, first):
                if not first:
                    dve.wait_ge(S["xT_ps"], b - 1)
                    dve.wait_ge(S["xn_kept"], b - 1)
                for j in range(2):
                    tile = bass.ds(b * 2 + j, 1)
                    dve.tensor_scalar(xn_slot[:, r, j, :], x_all[:, tile, :].rearrange("p o d -> p (o d)"),
                                      rstd[:, tile], nmr[:, tile], ALU.mult, ALU.add).then_inc(S["xn_done"], 1)

            def remainder(b, r, first):
                dve.wait_ge(S["part1_done"], b + 1)
                if not first:
                    dve.wait_ge(S["part3_done"], b - 1)
                dve.tensor_tensor(rem[:, r].rearrange("p (s t) -> p s t", s=2), bank[2 + r][:, :].rearrange("p (s t) -> p s t", s=2),
                                  parts[:, r, 0], ALU.subtract).then_inc(S["rem_done"], 1)
                dve.wait_ge(S["v_done"], b + 1)
                dve.tensor_tensor(logits[:, bass.ds(b * 2, 2), :], bank[4 + r][:, 0:NBLK * VL].rearrange("p (j x) -> p j x", x=2 * VL)[:, :, BLK:VL],
                                  br_sb[:, :].unsqueeze(1).to_broadcast([P, 2, E]), ALU.add).then_inc(S["lg_done"], 1)
            def unit_max(b, r, u, first_bank=0):
                n, pairs, ln_u = lens(u)
                dve.wait_ge(S["s_ps"], b * NU + u + 1)
                dve.tensor_reduce(row_max[r][:, n, pairs[0]:pairs[-1] + 1],
                                  bank[first_bank + (u + r) % 2][:, 0:ln_u * len(pairs)].rearrange("p (c k) -> p c k", k=ln_u),
                                  AX.X, ALU.max).then_inc(S["max_done"], 1)

            def max_parts(b, r, n):
                if n == 0:
                    dve.wait_ge(S["max_done"], (b + 1) * NU)
                    if has(b, 2, 15):
                        dve.wait_ge(S["mT_ps"], b - 1)
                    dve.tensor_scalar(nmax[r][:, :, 0, :], row_max[r][:, :, :], -1.0, None, ALU.mult).then_inc(S["nmax1"], 1)
                if n == 1:
                    dve.wait_ge(S["nmax1"], b + 1)
                    dve.scalar_tensor_tensor(nmax_rem[:, :, :], row_max[r][:, :, :], -1.0, nmax[r][:, :, 0, :],
                                             ALU.mult, ALU.subtract).then_inc(S["nmax_r"], 1)
                if n == 2:
                    dve.wait_ge(S["nmax_r"], b + 1)
                    dve.tensor_copy(nmax[r][:, :, 1, :], nmax_rem[:, :, :]).then_inc(S["nmax2"], 1)
                if n == 3:
                    dve.wait_ge(S["nmax2"], b + 1)
                    dve.tensor_tensor(nmax[r][:, :, 2, :], nmax_rem[:, :, :], nmax[r][:, :, 1, :], ALU.subtract).then_inc(S["nmax3"], 1)

            shape = [P, NT, E]
            m3 = [rt[:, c, :].rearrange("p (n e) -> p n e", e=E) for c in range(3)]

            def choose(b0, b1):
                n = slice(2 * b0, 2 * b1)
                some = [P, 2 * (b1 - b0), E]
                iota3 = iota8.unsqueeze(1).to_broadcast(some)
                dve.wait_ge(S["lg_done"], b1)
                then(dve.tensor_reduce(r32[:, 0, n], logits[:, n, :], AX.X, ALU.max))
                then(dve.tensor_tensor(m3[0][:, n, :], logits[:, n, :], r32[:, 0, n].unsqueeze(2).to_broadcast(some), ALU.is_equal))
                then(dve.tensor_tensor(m3[0][:, n, :], m3[0][:, n, :], iota3, ALU.mult))
                then(dve.tensor_reduce(r32[:, 1, n], m3[0][:, n, :], AX.X, ALU.min))
                dve.tensor_tensor(onehot_b[:, n, :], iota3, r32[:, 1, n].unsqueeze(2).to_broadcast(some), ALU.is_equal).then_inc(S["onehot_done"], 1)

            normalise(0, 0, True)
            normalise(1, 1, True)
            moments(1)
            for b in range(4):
                normalise(b + 2, b % 2, False)
                remainder(b, b % 2, b < 2)
                if b in (0, 3):
                    statistics(1 + b // 3)
                if b in (1, 2):
                    moments(b + 1)
            with dve.Fori(2, BESIDE // 2) as k:
                for r in range(2):
                    normalise(k * 2 + 2 + r, r, False)
                    remainder(k * 2 + r, r, False)
            for b in range(BESIDE, NB):
                if b + 2 < NB:
                    normalise(b + 2, b % 2, False)
                remainder(b, b % 2, False)
                if b == CHOSEN:
                    choose(0, CHOSEN)
                for n, u in EARLY_UNITS[b]:
                    unit_max(n, n, u, 6)
                    if (n, u) == (0, NU - 1):
                        for instruction in range(4):
                            max_parts(0, 0, instruction)

            choose(CHOSEN, NB)

            def segments():
                dve.wait_ge(S["rank_ps"], 2)
                dve.memset(r32[:, 2, :], 0.0)
                then(dve.tensor_scalar(r8[:, 0, :], bank[7][:, NT * E:(NT + 1) * E], float(P - 1), None, ALU.add))
                then(dve.tensor_copy(r8i[:, 0, :], r8[:, 0, :]))
                then(dve.tensor_scalar(r8i[:, 1, :], r8i[:, 0, :], P.bit_length() - 1, None, ALU.arith_shift_right))
                then(dve.tensor_copy(r8[:, 1, :], r8i[:, 1, :]))
                then(dve.tensor_tensor_scan(r8[:, 2, :], r8[:, 1, :], r32[:, 2, 0:E], 0.0, ALU.add, ALU.add))
                then(dve.tensor_tensor(r8[:, 3, :], r8[:, 2, :], r8[:, 1, :], ALU.subtract))
                then(dve.tensor_scalar(r8[:, 4, :], r8[:, 3, :], float(P), None, ALU.mult))

            def token_slots():
                then(dve.tensor_tensor(m3[1], bank[7][:, 0:NT * E].rearrange("p (n e) -> p n e", e=E),
                                       r8[:, 4, :].unsqueeze(1).to_broadcast(shape), ALU.add))
                then(dve.tensor_tensor(m3[2], m3[1], onehot_b[:, :, :], ALU.mult))
                then(dve.tensor_reduce(r32[:, 3, :], m3[2], AX.X, ALU.add))
                dve.tensor_copy(slot_of[:, :], r32[:, 3, :]).then_inc(S["slots_done"], 1)

            def tile_experts():
                te_shape = [1, SLOT_TILES, E]
                then(dve.tensor_tensor(te_cmp[:, :, :], iota_tile.unsqueeze(2).to_broadcast(te_shape),
                                       r8[0:1, 2, :].unsqueeze(1).to_broadcast(te_shape), ALU.is_ge))
                then(dve.tensor_reduce(te_f[:, 0, :], te_cmp[:, :, :], AX.X, ALU.add))
                then(dve.tensor_scalar(te_f[:, 1, :], te_f[:, 0, :], float(E - 1), None, ALU.min))
                dve.tensor_copy(tile_expert[:, :], te_f[:, 1, :]).then_inc(S["tile_expert_done"], 1)

            def divide(b, second):
                ov = bank[6][:, :].rearrange("p (c k) -> p c k", k=16)
                if not second:
                    dve.wait_ge(S["otok_ps"], b + 1)
                    dve.reciprocal(rz[:, :], ov[:, :, DH]).then_inc(S["rz_done"], 1)
                else:
                    dve.wait_ge(S["rz_done"], b + 1)
                    wait(dve, "o2T_ps", b)
                    dve.tensor_tensor(o_tok[:, :, :].rearrange("p j (c d) -> p (j c) d", d=DH), ov[:, :, 0:DH],
                                      rz[:, :].unsqueeze(2).to_broadcast([P, 2 * H, DH]), ALU.mult).then_inc(S["otok_done"], 1)

            def gate_recip(i, r, u):
                c, n = (GATE_STEPS.index(i), GATE_CHUNKS[i][1] - GATE_CHUNKS[i][0]) if isinstance(i, int) else (i - GATE_STEP, GATE_TILES)
                e = gate_e[r][:, 0:n * D]
                if u in GATE_PIECES:
                    dve.wait_ge(S["gate_sum_done"], c + 1)
                    w, q = n * D // len(GATE_PIECES), GATE_PIECES.index(u)
                    piece = e[:, q * w:(q + 1) * w]
                    dve.reciprocal(piece, piece).then_inc(S["gate_recip_done"], 1)

            ROUTING = {3: segments, 4: token_slots, 8: tile_experts}

            def step(i, r, gate):
                for u in range(NU):
                    if has(i, 0, 13):
                        unit_max(i + 2, r, u)
                    if u < 4 and has(i, 0, 14):
                        max_parts(i + 1, 1 - r, u)
                    if u in (3, 4) and has(i, 1, 15):
                        divide(i - 1, u == 4)
                    if gate:
                        gate_recip(i, r, u)
                    if isinstance(i, int) and i == 0 and u in ROUTING:
                        ROUTING[u]()

            def relu(t, r):
                dve.wait_ge(S["h_ps"], t + 1)
                wait(dve, "y_ps", t - 2)
                for c in range(NC_H):
                    last = dve.tensor_scalar(hT[:, r, c, :], bank[r][:, c * P:(c + 1) * P], w_slot[r][:, WE + c:WE + c + 1],
                                             w_slot[r][:, WE + NC_H + c:WE + NC_H + c + 1], ALU.max, ALU.add)
                last.then_inc(S["h_done"], 1)

            def keep_y(t, r, turn):
                dve.wait_ge(S["y_ps"], t + 1)
                if turn is not None:
                    dve.wait_ge(S[f"y_out{r}"], turn * 16)
                dve.tensor_copy(y_slot[:, r, :], bank[3 + r][:, 0:D]).then_inc(S["y_done"], 1)

            def experts():
                dve.wait_ge(S["experts_in"], 16 * E)
                b1 = w_all[:, :, HID + NC_H * D:WE]
                dve.tensor_scalar(w_all[:, :, WE:WE + NC_H], b1, -1.0, None, ALU.mult).then_inc(S["bias_done"], 1)
                dve.tensor_scalar(w_all[:, :, WE + NC_H:WB], b1, 0.0, None, ALU.min).then_inc(S["bias_done"], 1)
                relu(0, 0)
                for t in (1, 2):
                    relu(t, t)
                    keep_y(t - 1, t - 1, None)
                relu(3, 0)
                keep_y(2, 2, None)
                for t in (4, 5):
                    relu(t, t - 3)
                    keep_y(t - 1, t - 4, 1)
                with dve.Fori(2, TURNS) as k:
                    relu(k * 3, 0)
                    keep_y(k * 3 - 1, 2, k - 1)
                    for r in (1, 2):
                        relu(k * 3 + r, r)
                        keep_y(k * 3 + r - 1, r - 1, k)
                keep_y(SLOT_TILES - 1, 2, TURNS - 1)
            attention_steps(step, dve, experts)
            divide(NB - 1, False)
            divide(NB - 1, True)
            tiles = slice(NT - 2, NT)
            dve.wait_ge(S["s_out_ps"], NB)
            dve.wait_ge(S["gate_done"], len(GATE_STEPS))
            then(dve.tensor_tensor(s_all[:, tiles, :], bank[7][:, 2 * P:4 * P].rearrange("p (j d) -> p j d", d=D),
                                   y_tok[:, tiles, :], ALU.mult))
            dve.tensor_tensor(s_all[:, tiles, :], s_all[:, tiles, :], x_all[:, tiles, :], ALU.add).then_inc(S["last_done"], 1)

        @block.tensor
        def _(pe):
            pe.wait_ge(S["zero_src"], 1)
            cold = zeros[:, :].bitcast(BF16)
            for n in range(16):
                pe.matmul(bank[7][:, :], cold[:, 0:P], cold.unsqueeze(1).to_broadcast([P, 2, 2 * D]), start=True, stop=True)
            pe.wait_ge(S["weights_in"], 16 * 5)
            for n in range(3):
                last = pe.matmul(bank[0][:, n * P:(n + 1) * P], lora_b[:, n, :], lora_a[:, n, :], start=(n == 0), stop=True,
                                 skip_group_check=True)
            last.then_inc(S["lora_ps"], 1)
            pe.wait_ge(S["w_eff_done"], 1)

            last_odd = (next(b for b, units in EARLY_UNITS.items() if (1, 1) in units) - 1) // 2 * 2 + 1

            def turn(b, r, first):
                pe.wait_ge(S["xn_done"], 2 * b + 2)
                if not first:
                    pe.wait_ge(S["xT_done"], b - 1)
                for j in range(2):
                    last = pe.transpose(bank[r][:, j * P:(j + 1) * P], xn_slot[:, r, j, :], ident_f)
                last.then_inc(S["xT_ps"], 1)

            def project(b, r, first):
                pe.wait_ge(S["xT_done"], b + 1)
                if not first:
                    pe.wait_ge(S["rem_done"], b - 1)
                by_block = xnT_slot[:, r, :].rearrange("p (k i) -> p i k", k=NBLK)
                for n in range(2):
                    last = pe.matmul(bank[2 + r][:, n * T:(n + 1) * T], w_eff[:, n, :], by_block, start=(n == 0),
                                     stop=True, skip_group_check=True)
                last.then_inc(S["qk_ps"], 1)
                if not first:
                    pe.wait_ge(S["v_done"], b - 1)
                    pe.wait_ge(S["lg_done"], b - 1)
                if isinstance(b, int) and b == last_odd + 2:
                    pe.wait_ge(S["nmaxT_done"], 1)
                for n in range(NBLK):
                    for a in range(2):
                        w0, w1 = ((0, BLK + E), (BLK, 2 * BLK + E))[a] if a == n % 2 else ((0, BLK), (BLK + E, 2 * BLK + E))[a]
                        c0 = n * VL + w0 - a * (BLK + E)
                        last = pe.matmul(bank[4 + r][64 * a:64 * a + 64, c0:c0 + w1 - w0], xnT_slot[:, r, n * BLK:(n + 1) * BLK],
                                         w_v_flat[:, w0:w1], start=(n == 0), stop=True, skip_group_check=True)
                last.then_inc(S["lg_ps"], 1)

            def count_in_tiles():
                pe.wait_ge(S["onehot_done"], 2)
                oh = onehot_b[:, :, :].rearrange("p n e -> p (n e)")
                pe.matmul(bank[7][:, 0:NT * E], before_b, oh, start=True, stop=False, skip_group_check=True)
                for h in range(2):
                    last = pe.matmul(bank[7][:, 384 + h:385 + h], oh[:, h * P:(h + 1) * P], one_b, start=False, stop=True, skip_group_check=True)
                last.then_inc(S["rank_ps"], 1)

            def count_before():
                pe.wait_ge(S["counts_done"], 1)
                for h in range(2):
                    for c0, c1 in ((0, NT * E), (NT * E, (NT + 1) * E)):
                        last = pe.matmul(bank[7][:, c0:c1], tile_counts[:, h, :], later_b[:, h, c0:c1], start=False, stop=(h == 1), skip_group_check=True)
                last.then_inc(S["rank_ps"], 1)

            def blocks(columns, low, high):
                return columns.rearrange("p (i k) -> p i k", k=NBLK)[:, :, low:high]

            def max_scores(b, r, u, first_bank=0):
                n, pairs, ln_u = lens(u)
                if u == 0:
                    pe.wait_ge(S[f"qd_ks_in{r}"], (b - r) * (LOADS * 8) + LOADS * 16)
                wait(pe, "max_done", b * NU + u - 1)
                ps = bank[first_bank + (u + r) % 2]
                for c, p in enumerate(pairs):
                    pe.matmul(ps[:, c * ln_u:(c + 1) * ln_u], q_diag[r][:, p].rearrange("x h t -> x (h t)")[:, n::NBLK], blocks(k_plain[r][:, p, :], 0, n + 1),
                              start=(c == 0), stop=False, skip_group_check=True)
                pe.matmul(ps[:, 0:ln_u * len(pairs)].rearrange("p (c k) -> p c k", k=ln_u)[:, :, n::n + 1], ident_b,
                          mask_qk.unsqueeze(1).to_broadcast([P, len(pairs), BLK]), start=False, stop=True,
                          skip_group_check=True).then_inc(S["s_ps"], 1)

            def scores(b, r, u):
                n, pairs, ln_u = lens(u)
                kb = NBLK - 1 - n
                if u == 0:
                    pe.wait_ge(S[f"qs_kd_in{r}"], (b - r) * (LOADS * 8) + LOADS * 16)
                    pe.wait_ge(S[f"max_in{r}"], (b - r) * 16 + 32)
                if in_four_banks(b):
                    wait(pe, "exp_done", b * NU + u - 3)
                    pe.wait_ge(S["max_done"], NB * NU)
                else:
                    wait(pe, "exp_done", b * NU + u - 1)
                ps = score_bank(b, r, u)
                for c, p in enumerate(pairs):
                    pe.matmul(ps[:, c * ln_u:(c + 1) * ln_u], k_diag[r][:, p].rearrange("x h t -> x (h t)")[:, kb::NBLK], blocks(q_plain[r][:, p, :], kb, NBLK),
                              start=(c == 0), stop=False, skip_group_check=True)
                pe.matmul(ps[:, 0:ln_u * len(pairs)].rearrange("p (c k) -> p c k", k=ln_u)[:, :, 0::n + 1], ident_b,
                          mask_kq.unsqueeze(1).to_broadcast([P, len(pairs), BLK]), start=False, stop=True,
                          skip_group_check=True).then_inc(S["st_ps"], 1)

            def values(b, r, u):
                if u == 1:
                    pe.wait_ge(S["vdiag_done"], b + 1)
                    wait(pe, "oT_done", b)
                pe.wait_ge(S["exp_done"], b * NU + u + 1)
                for w in PV_AFTER[u]:
                    n, pairs, ln_u = lens(w)
                    kb = NBLK - 1 - n
                    for c, p in enumerate(pairs):
                        j, g = p % 4, p // 4
                        by_block = bank[4][32 * j:32 * j + 32, g * T:(g + 1) * T].rearrange("p (k i) -> p i k", k=NBLK)
                        last = pe.matmul(by_block[:, :, kb:NBLK], v_diag[r][:, kb, p, :],
                                         probs[:, w, c * ln_u:(c + 1) * ln_u], start=(kb == 0 and g == 0), stop=(kb == NBLK - 1),
                                         skip_group_check=True)
                last.then_inc(S["pv_ps"], 1)

            def turn_max(b, r):
                pe.wait_ge(S["nmax3"], b + 1)
                wait(pe, "nmaxT_done", b)
                for n in range(NBLK):
                    last = pe.matmul(bank[5][0:3 * NP, n::NBLK], nmax[r][:, n].rearrange("p c h -> p (c h)"), ident_b, start=(n == 0),
                                     stop=True, skip_group_check=True)
                last.then_inc(S["mT_ps"], 1)

            def turn_o(b):
                pe.wait_ge(S["oT_done"], b + 1)
                wait(pe, "otok_done", b)
                for j in range(2):
                    for g in range(2):
                        last = pe.transpose(bank[6][:, (j * 2 + g) * P:(j * 2 + g + 1) * P], oT[:, g * T + j * P:g * T + (j + 1) * P], ident_f)
                last.then_inc(S["otok_ps"], 1)

            def turn_o_back(b):
                pe.wait_ge(S["otok_done"], b + 1)
                wait(pe, "s_done", b)
                for j in range(2):
                    last = pe.transpose(bank[7][:, j * P:(j + 1) * P], o_tok[:, j, :], ident_f)
                last.then_inc(S["o2T_ps"], 1)

            def out_project(b):
                pe.wait_ge(S["o2T_done"], b + 1)
                for j in range(2):
                    last = pe.matmul(bank[7][:, (2 + j) * P:(3 + j) * P], o2T[:, j * P:(j + 1) * P], wp_sb[:, :],
                                     start=True, stop=True, skip_group_check=True)
                last.then_inc(S["s_out_ps"], 1)

            def early(n, u):
                max_scores(n, n, u, 6)
                if (n, u) == (1, 1):
                    pe.wait_ge(S["v_done"], last_odd + 1)
                    pe.wait_ge(S["lg_done"], last_odd + 1)
                    turn_max(0, 0)
            projection_steps(turn, project, pe, None, early)
            pe.wait_ge(S["xT_done"], NB)
            pe.wait_ge(S["rem_done"], NB)
            pe.wait_ge(S["v_done"], NB)
            pe.wait_ge(S["lg_done"], NB)

            def step(i, r, gate):
                for u in range(NU):
                    if not in_four_banks(i):
                        scores(i, r, u)
                    else:
                        for w in ((0, 1, 2) if (i, u) == (NB - 2, 0) else (u + 2,)):
                            if w < NU:
                                scores(i, r, w)
                            elif i < NB - 1:
                                scores(i + 1, 1 - r, w - NU)
                    if has(i, 0, 13):
                        max_scores(i + 2, r, u)
                    if u - 1 in PV_AFTER:
                        values(i, r, u - 1)
                    if has(i, 0, 14) and u == max_at(i):
                        turn_max(i + 1, 1 - r)
                    if isinstance(i, int) and i == 0 and u == 1:
                        count_in_tiles()
                    if isinstance(i, int) and i == 0 and u == 2:
                        count_before()
                    if has(i, 1, 15):
                        if u == 1:
                            turn_o(i - 1)
                        if u == 6:
                            turn_o_back(i - 1)
                        if u == NU - 1:
                            out_project(i - 1)
                values(i, r, NU - 1)

            def experts():
                b = EXPERTS_AFTER
                pe.wait_ge(S["max_done"], (b + 3) * NU)
                pe.wait_ge(S["exp_done"], (b + 1) * NU)
                pe.wait_ge(S["s_done"], b)

                def turn_rows(t, r, turn):
                    pe.wait_ge(S[f"xs_in{r}"], turn * 16 + 16)
                    wait(pe, "xsT_done", t)
                    pe.transpose(bank[6][:, r * P:(r + 1) * P], xs_slot[:, r, :], ident_f).then_inc(S["xsT_ps"], 1)

                def hidden(t, r):
                    pe.wait_ge(S["xsT_done"], t + 1)
                    pe.wait_ge(S["w_done"], t + 1)
                    wait(pe, "h_done", t - 2)
                    for c in range(NC_H):
                        last = pe.matmul(bank[r][:, c * P:(c + 1) * P], w_slot[r][:, c * P:(c + 1) * P],
                                         xsT_slot[:, r, :], start=(c == 0),
                                         stop=True, skip_group_check=True)
                    last.then_inc(S["h_ps"], 1)

                def output(t, r):
                    pe.wait_ge(S["h_done"], t + 1)
                    wait(pe, "y_done", t - 2)
                    for c in range(NC_H):
                        last = pe.matmul(bank[3 + r][:, 0:D], hT[:, r, c, :], w_slot[r][:, HID + c * D:HID + (c + 1) * D],
                                         start=(c == 0), stop=(c == NC_H - 1))
                    last.then_inc(S["y_ps"], 1)
                def add_row():
                    pe.wait_ge(S["c_sum"], 1 + SUM_STEPS)
                    pe.matmul(bank[7][:, 0:D], ones_f, xn_all[:, 0, :], start=True, stop=False)
                    pe.matmul(bank[7][:, 0:D], ones_f[0:E, :], b2_sb, start=False, stop=True).then_inc(S["c_bc_ps"], 1)

                turn_rows(0, 0, 0)
                turn_rows(1, 1, 0)
                hidden(0, 0)
                turn_rows(2, 2, 0)
                pe.wait_ge(S["oT_done"], b + 1)
                pe.wait_ge(S["nmaxT_done"], b + 2)
                for t in (1, 2):
                    hidden(t, t)
                    turn_rows(t + 2, t - 1, 1)
                    output(t - 1, t - 1)
                with pe.Fori(1, TURNS - 1) as k:
                    for r in range(3):
                        hidden(k * 3 + r, r)
                        turn_rows(k * 3 + r + 2, (r + 2) % 3, k + (r + 2) // 3)
                        output(k * 3 + r - 1, (r + 2) % 3)
                add_row()
                for t in range(SLOT_TILES - 3, SLOT_TILES):
                    hidden(t, t % 3)
                    if t + 2 < SLOT_TILES:
                        turn_rows(t + 2, (t + 2) % 3, (t + 2) // 3)
                    output(t - 1, (t - 1) % 3)
                output(SLOT_TILES - 1, 2)
                pe.wait_ge(S["c_bc_done"], 1)
                pe.wait_ge(S["y_done"], SLOT_TILES)
            attention_steps(step, pe, experts)
            turn_o(NB - 1)
            turn_o_back(NB - 1)
            out_project(NB - 1)


def shape_constants():
    def bf16_bits(a):
        u = np.asarray(a, np.float32).view(np.uint32)
        return ((u + 0x7fff + ((u >> 16) & 1)) >> 16).astype(np.uint16)

    def value(bits):
        return (bits.astype(np.uint32) << 16).view(np.float32)

    f = np.zeros((P, 2 * P + 64), np.float32)
    f[:, 0:P] = np.eye(P)
    f[:, P:2 * P] = 1.0
    f[:, 2 * P:2 * P + E] = np.arange(E) - E
    f[:, 2 * P + 8:2 * P + 8 + SLOT_TILES] = np.arange(SLOT_TILES)
    f[0:BLK, 2 * P + 50] = 1
    f[BLK:, 2 * P + 51] = 1
    i, j = np.arange(P)[:, None] % BLK, np.arange(BLK)[None, :]
    n, m = np.arange(P)[:, None], np.arange(P)[None, :]
    rows, columns = np.arange(NT * E)[:, None], np.arange((NT + 1) * E)[None, :]
    later = (rows % E == columns % E) & (rows // E < columns // E)
    later = later.reshape(2, P, (NT + 1) * E).transpose(1, 0, 2).reshape(P, 2 * (NT + 1) * E)
    b = np.concatenate([np.where(j > i, NEG, 0), np.where(j < i, NEG, 0), n == m, n < m, later, np.ones((P, 2))], axis=1)
    start = 2.0 ** (-2.0 ** (-(np.log2(H) - 3)))
    slope = np.array([start * start ** h for h in range(H)], np.float32).astype(np.float64)
    rise = slope.reshape(NP, 2).T[:, :, None] * (np.arange(T) % NBLK * BLK + np.arange(T) // NBLK)
    rise = rise.reshape(2, NP * T)
    cut, rest = [], rise
    for _ in range(3):
        cut.append(value(bf16_bits(rest)))
        rest = rest - cut[-1].astype(np.float64)
    q, k = np.zeros((2, 16, NP * T)), np.zeros((2, 16, NP * T))
    for c in range(3):
        q[:, c], k[:, c] = 1, -cut[c]
        q[:, 3 + c], k[:, 3 + c] = cut[c], 1
        k[:, 6 + c] = 1
    q, k = (np.concatenate([a, a], axis=2) for a in (q, k))
    return f, bf16_bits(b), bf16_bits(q), bf16_bits(k)


def kernel(L0_attn_x, L0_attn_Wq, L0_attn_Aq, L0_attn_Bq, L0_attn_Wk, L0_attn_Ak, L0_attn_Bk, L0_attn_Wv, L0_attn_Av,
           L0_attn_Bv, L0_attn_Wp, L0_ffn_W1, L0_ffn_b1, L0_ffn_W2, L0_ffn_b2, L0_ffn_Wr, L0_ffn_br):
    import concourse.bacc as bacc
    from concourse.bass_utils import run_bass_kernel_spmd

    def pair_order(w):
        w = np.asarray(w)
        return w.reshape(w.shape[0], NP, 2, DH).transpose(0, 2, 3, 1).reshape(w.shape[0], H * DH)

    def halves(w):
        w = np.asarray(w)
        return w.reshape(w.shape[0], NP, 2, DH).transpose(0, 2, 1, 3).reshape(w.shape[0], H * DH)

    w1, w2, b1 = (np.asarray(a) for a in (L0_ffn_W1, L0_ffn_W2, L0_ffn_b1))
    w_experts = np.concatenate([w1, w2.reshape(E, NC_H, P, D).transpose(0, 2, 1, 3).reshape(E, P, NC_H * D),
                                b1.reshape(E, NC_H, P).transpose(0, 2, 1)], axis=2)
    const_f32, const_bf16, q_rows, k_rows = shape_constants()
    arrays = {
        "x": L0_attn_x,
        "w_dense": np.concatenate([pair_order(np.asarray(L0_attn_Wq).T), pair_order(np.asarray(L0_attn_Wk).T), halves(np.asarray(L0_attn_Wv).T),
                                   np.asarray(L0_attn_Wp).T, np.asarray(L0_ffn_Wr)], axis=1),
        "lora": np.concatenate([pair_order(np.asarray(L0_attn_Aq).T), pair_order(np.asarray(L0_attn_Ak).T), halves(np.asarray(L0_attn_Av).T),
                                *(np.asarray(a) for a in (L0_attn_Bq, L0_attn_Bk, L0_attn_Bv, L0_ffn_b2))], axis=1),
        "br": L0_ffn_br, "w_experts": w_experts,
        "const_f32": const_f32, "const_bf16": const_bf16, "q_const_rows": q_rows, "k_const_rows": k_rows,
    }
    arrays = {n: np.ascontiguousarray(a) for n, a in arrays.items()}
    nc = bacc.Bacc("TRN2", target_bir_lowering=False, num_devices=1)
    args = [nc.dram_tensor(n, a.shape, mybir.dt.from_np(a.dtype), kind="ExternalInput").ap() for n, a in arrays.items()]
    out = nc.dram_tensor("out", (NB, T, D), F32, kind="ExternalOutput").ap()
    program(nc, *args, out)
    r = run_bass_kernel_spmd(nc, [arrays], core_ids=[0])
    return r.results[0]["out"]
```
